# Optimizing a Trainium2 kernel written in Bass

```python
import numpy as np
import jax
import jax.numpy as jnp

def _softmax(x, axis=-1):
    return jax.nn.softmax(x, axis=axis)

def _gelu(x):
    return jax.nn.gelu(x, approximate=True)

def _silu(x):
    return jax.nn.silu(x)

def _sigmoid(x):
    return jax.nn.sigmoid(x)

def _layernorm(x, axis=-1, eps=1e-05):
    m = jnp.mean(x, axis=axis, keepdims=True)
    v = jnp.var(x, axis=axis, keepdims=True)
    return (x - m) / jnp.sqrt(v + eps)

def _scatter_add(tgt, idx, src, axis=0):
    return tgt.at[idx].add(src)

def _segment_sum(src, seg, n):
    return jax.ops.segment_sum(src, seg, n)
kernel_name = 'mk_recurrent_d1_jaxref_r2_ae2d22'

def setup_inputs(seed: int=0):
    np.random.seed(seed)
    _w = jnp.asarray

    def _L0_attn_setup():
        import jax, jax.numpy as jnp
        import numpy as np
        import math
        D = 1024
        H = 32
        HKV = 8
        HD = D // H
        ROPE_BASE = 10000.0

        def _rope_cache(T, hd, base=ROPE_BASE):
            theta = 1.0 / base ** (jnp.arange(0, hd, 2, dtype=jnp.float32) / hd)
            t = jnp.arange(T, dtype=jnp.float32)
            freqs = t[:, None] * theta[None, :]
            return (jnp.cos(freqs), jnp.sin(freqs))

        def _apply_rope(x, cos, sin):
            B, Hh, T, hd = x.shape
            x_ = x.reshape(B, Hh, T, hd // 2, 2)
            x1, x2 = (x_[..., 0], x_[..., 1])
            c = cos[None, None, :, :]
            s = sin[None, None, :, :]
            rx1 = x1 * c - x2 * s
            rx2 = x1 * s + x2 * c
            return jnp.stack([rx1, rx2], axis=-1).reshape(B, Hh, T, hd)
        key = jax.random.key(seed)
        ks = jax.random.split(key, 5)
        B, T = (1, 1024)
        sc = 0.02
        return {'x': jax.random.normal(ks[0], (B, T, D), dtype=jnp.float32), 'wq': jax.random.normal(ks[1], (D, D), dtype=jnp.float32) * sc, 'wk': jax.random.normal(ks[2], (HKV * HD, D), dtype=jnp.float32) * sc, 'wv': jax.random.normal(ks[3], (HKV * HD, D), dtype=jnp.float32) * sc, 'wo': jax.random.normal(ks[4], (D, D), dtype=jnp.float32) * sc}
    _L0_attn_in = _L0_attn_setup()

    def _L0_ffn_setup():
        import jax, jax.numpy as jnp
        import numpy as np
        EPS = 1e-06
        K_STEPS = 4
        USE_GATING = True

        def layer_norm(x, gamma, beta):
            mu = jnp.mean(x, axis=-1, keepdims=True)
            var = jnp.mean(jnp.square(x - mu), axis=-1, keepdims=True)
            return (x - mu) * jax.lax.rsqrt(var + EPS) * gamma + beta
        key = jax.random.key(seed)
        B, L, D, H = (4, 2048, 1024, 4096)
        ks = jax.random.split(key, 16)
        s = 0.02
        return {'x': jax.random.normal(ks[0], (B, L, D), dtype=jnp.float32), 'in_gamma': jnp.ones((D,), jnp.float32), 'in_beta': jnp.zeros((D,), jnp.float32), 'agg_w': jax.random.normal(ks[1], (D, D), jnp.float32) * s, 'agg_b': jnp.zeros((D,), jnp.float32), 'pn_gamma': jnp.ones((D,), jnp.float32), 'pn_beta': jnp.zeros((D,), jnp.float32), 'd1_w': jax.random.normal(ks[2], (D, H), jnp.float32) * s, 'd1_b': jnp.zeros((H,), jnp.float32), 'd2_w': jax.random.normal(ks[3], (H, D), jnp.float32) * s, 'd2_b': jnp.zeros((D,), jnp.float32), 'bc_w': jax.random.normal(ks[4], (D, D), jnp.float32) * s, 'bc_b': jnp.zeros((D,), jnp.float32), 'gate_w': jax.random.normal(ks[5], (D, D), jnp.float32) * s, 'gate_b': jnp.zeros((D,), jnp.float32), 'out_gamma': jnp.ones((D,), jnp.float32), 'out_beta': jnp.zeros((D,), jnp.float32)}
    _L0_ffn_in = _L0_ffn_setup()
    _d = {'L0_attn_x': _L0_attn_in['x'], 'L0_attn_wq': _L0_attn_in['wq'], 'L0_attn_wk': _L0_attn_in['wk'], 'L0_attn_wv': _L0_attn_in['wv'], 'L0_attn_wo': _L0_attn_in['wo'], 'L0_ffn_in_gamma': _L0_ffn_in['in_gamma'], 'L0_ffn_in_beta': _L0_ffn_in['in_beta'], 'L0_ffn_agg_w': _L0_ffn_in['agg_w'], 'L0_ffn_agg_b': _L0_ffn_in['agg_b'], 'L0_ffn_pn_gamma': _L0_ffn_in['pn_gamma'], 'L0_ffn_pn_beta': _L0_ffn_in['pn_beta'], 'L0_ffn_d1_w': _L0_ffn_in['d1_w'], 'L0_ffn_d1_b': _L0_ffn_in['d1_b'], 'L0_ffn_d2_w': _L0_ffn_in['d2_w'], 'L0_ffn_d2_b': _L0_ffn_in['d2_b'], 'L0_ffn_bc_w': _L0_ffn_in['bc_w'], 'L0_ffn_bc_b': _L0_ffn_in['bc_b'], 'L0_ffn_gate_w': _L0_ffn_in['gate_w'], 'L0_ffn_gate_b': _L0_ffn_in['gate_b'], 'L0_ffn_out_gamma': _L0_ffn_in['out_gamma'], 'L0_ffn_out_beta': _L0_ffn_in['out_beta']}
    _x0 = _d['L0_attn_x']
    _d['L0_attn_x'] = jax.random.normal(jax.random.fold_in(jax.random.key(seed), 1), (4, 1024, 1024), dtype=_x0.dtype)
    del _x0
    return _d

def reference(L0_attn_x, L0_attn_wq, L0_attn_wk, L0_attn_wv, L0_attn_wo, L0_ffn_in_gamma, L0_ffn_in_beta, L0_ffn_agg_w, L0_ffn_agg_b, L0_ffn_pn_gamma, L0_ffn_pn_beta, L0_ffn_d1_w, L0_ffn_d1_b, L0_ffn_d2_w, L0_ffn_d2_b, L0_ffn_bc_w, L0_ffn_bc_b, L0_ffn_gate_w, L0_ffn_gate_b, L0_ffn_out_gamma, L0_ffn_out_beta):

    def _L0_attn_ref(x, wq, wk, wv, wo):
        import jax, jax.numpy as jnp
        import numpy as np
        import math
        D = 1024
        H = 32
        HKV = 8
        HD = D // H
        ROPE_BASE = 10000.0

        def _rope_cache(T, hd, base=ROPE_BASE):
            theta = 1.0 / base ** (jnp.arange(0, hd, 2, dtype=jnp.float32) / hd)
            t = jnp.arange(T, dtype=jnp.float32)
            freqs = t[:, None] * theta[None, :]
            return (jnp.cos(freqs), jnp.sin(freqs))

        def _apply_rope(x, cos, sin):
            B, Hh, T, hd = x.shape
            x_ = x.reshape(B, Hh, T, hd // 2, 2)
            x1, x2 = (x_[..., 0], x_[..., 1])
            c = cos[None, None, :, :]
            s = sin[None, None, :, :]
            rx1 = x1 * c - x2 * s
            rx2 = x1 * s + x2 * c
            return jnp.stack([rx1, rx2], axis=-1).reshape(B, Hh, T, hd)
        B, T, _ = x.shape
        q = (x @ wq.T).reshape(B, T, H, HD).transpose(0, 2, 1, 3)
        k = (x @ wk.T).reshape(B, T, HKV, HD).transpose(0, 2, 1, 3)
        v = (x @ wv.T).reshape(B, T, HKV, HD).transpose(0, 2, 1, 3)
        cos, sin = _rope_cache(T, HD)
        q = _apply_rope(q, cos, sin)
        k = _apply_rope(k, cos, sin)
        rep = H // HKV
        k = jnp.repeat(k, rep, axis=1)
        v = jnp.repeat(v, rep, axis=1)
        scores = jnp.einsum('bhtd,bhsd->bhts', q, k) / math.sqrt(HD)
        mask = jnp.triu(jnp.full((T, T), -jnp.inf, dtype=scores.dtype), k=1)
        scores = scores + mask[None, None, :, :]
        attn = jax.nn.softmax(scores, axis=-1)
        y = jnp.einsum('bhts,bhsd->bhtd', attn, v)
        y = y.transpose(0, 2, 1, 3).reshape(B, T, D)
        return y @ wo.T

    def _L0_ffn_ref(x, in_gamma, in_beta, agg_w, agg_b, pn_gamma, pn_beta, d1_w, d1_b, d2_w, d2_b, bc_w, bc_b, gate_w, gate_b, out_gamma, out_beta):
        import jax, jax.numpy as jnp
        import numpy as np
        EPS = 1e-06
        K_STEPS = 4
        USE_GATING = True

        def layer_norm(x, gamma, beta):
            mu = jnp.mean(x, axis=-1, keepdims=True)
            var = jnp.mean(jnp.square(x - mu), axis=-1, keepdims=True)
            return (x - mu) * jax.lax.rsqrt(var + EPS) * gamma + beta
        x_norm = layer_norm(x, in_gamma, in_beta)
        thought = x_norm[:, -1, :] @ agg_w + agg_b
        for _ in range(K_STEPS):
            t = layer_norm(thought, pn_gamma, pn_beta)
            t = jax.nn.gelu(t @ d1_w + d1_b, approximate=False)
            thought = thought + (t @ d2_w + d2_b)
        broadcast = (thought @ bc_w + bc_b)[:, None, :]
        if USE_GATING:
            gate = jax.nn.sigmoid(x @ gate_w + gate_b)
            out = x + gate * broadcast
        else:
            out = x + broadcast
        return layer_norm(out, out_gamma, out_beta)
    x = L0_attn_x
    xn = _layernorm(x, axis=-1)
    s = _L0_attn_ref(xn, L0_attn_wq, L0_attn_wk, L0_attn_wv, L0_attn_wo)
    g = _silu(_L0_ffn_ref(xn, L0_ffn_in_gamma, L0_ffn_in_beta, L0_ffn_agg_w, L0_ffn_agg_b, L0_ffn_pn_gamma, L0_ffn_pn_beta, L0_ffn_d1_w, L0_ffn_d1_b, L0_ffn_d2_w, L0_ffn_d2_b, L0_ffn_bc_w, L0_ffn_bc_b, L0_ffn_gate_w, L0_ffn_gate_b, L0_ffn_out_gamma, L0_ffn_out_beta))
    x = x + s * g
    return x

_drawn_inputs = setup_inputs


def setup_inputs(seed=0):
    import zlib

    import numpy as np

    out = dict(_drawn_inputs(seed))
    spreads = {'L0_ffn_in_gamma': (1.0, 0.6),
     'L0_ffn_in_beta': (0.0, 0.8),
     'L0_ffn_agg_b': (0.0, 2.0),
     'L0_ffn_pn_gamma': (1.0, 0.6),
     'L0_ffn_pn_beta': (0.0, 0.8),
     'L0_ffn_d1_b': (0.0, 0.8),
     'L0_ffn_d2_b': (0.0, 2.0),
     'L0_ffn_bc_b': (0.0, 2.0),
     'L0_ffn_gate_b': (0.0, 0.8),
     'L0_ffn_out_gamma': (1.0, 0.6),
     'L0_ffn_out_beta': (0.0, 0.8)}
    factors = {'L0_attn_wq': 5.736,
     'L0_attn_wk': 5.061,
     'L0_ffn_agg_w': 4.787,
     'L0_ffn_d1_w': 4.781,
     'L0_ffn_d2_w': 4.307,
     'L0_ffn_bc_w': 4.025,
     'L0_ffn_gate_w': 8.0}
    for name, (base, spread) in spreads.items():
        noise = np.random.default_rng([zlib.crc32(name.encode()), seed]).standard_normal(out[name].shape)
        drawn = base * np.exp(spread * noise) if base else spread * noise
        out[name] = jnp.asarray(drawn.astype(out[name].dtype))
    for name, factor in factors.items():
        out[name] = (out[name] * factor).astype(out[name].dtype)
    return out
```

```python
from contextlib import ExitStack

import numpy as np

import concourse.bass as bass
from concourse import mybir

F32 = mybir.dt.float32
F32R = mybir.dt.float32r
F16 = mybir.dt.float16
BF16 = mybir.dt.bfloat16
ALU = mybir.AluOpType
ACT = mybir.ActivationFunctionType
AX = mybir.AxisListType

P = 128
B, T, D = 4, 1024, 1024
H, KV, HD = 32, 8, 32
REP = H // KV
FF = 4096
STEPS = 4
KT = D // P
NT = T // P
HALF = T // 2
EO = HD // 2
PAIRS = H // 8
GROUPS = B * KV
CH = FF // D
VW = 3 * HD + 2
SCALE = HD ** -0.5
LIFT = float(np.log(256.0) / SCALE)
NEG = -1.0e30
EPS_X, EPS_F = 1e-5, 1e-6


def f32(ap):
    return ap.bitcast(F32)


def score_units(half):
    j0, q0 = 4 * half, HALF * half
    full = [([(j, q0, HALF, 0)], [], (0, HALF), HALF * j) for j in range(j0)]
    at = HALF * j0
    return full + [
        ([(j0, q0, 512, 0)], [0], (0, 512), at),
        ([(j0 + 1, q0 + 128, 384, 0)], [0], (0, 384), at + 512),
        ([(j0 + 3, q0 + 256, 256, 0), (j0 + 2, q0 + 256, 256, 256)], [128, 256], (128, 512), at + 896),
    ]


def prob_column(i, j):
    half, j0 = i // 4, 4 * (i // 4)
    if j < j0:
        return HALF * j + P * (i - j0)
    return HALF * j0 + [P * (i - j0), 512 + P * (i - j0 - 1), 1024 + P * (i - j0 - 2), 896][j - j0]


PROB_W = [1280, 3328]
ST = [(half, h, u) for half in range(2) for h in range(REP) for u in score_units(half)]
NST = len(ST)
HALF_ST = REP * 3


def max_units():
    out = []
    for i in range(NT):
        per = 4 if i < 2 else 2 if i < 4 else 1
        out += [(i, h, per) for h in range(0, REP, per)]
    return out


MX = max_units()
NMX = len(MX)
MX_HALF = sum(1 for i, _, _ in MX if i < 4)


def group_plan():
    at = [[] for _ in range(NST)]
    late = [(i, h) for i in range(4, 8) for h in range(REP)]
    for k, (i, h) in enumerate(late):
        at[k * 11 // 16].append(("pv", 1, i, h))
    early = [(i, h) for i in range(4) for h in range(REP)]
    for k, (i, h) in enumerate(early):
        at[16 + k].append(("pv", 0, i, h))
    for k in range(NMX):
        at[10 + k * 28 // NMX].append(("mx", k))
    at[2].append(("mt", 1))
    at[5].append(("fa",))
    at[13].append(("yt", 1))
    at[20].append(("mt", 0))
    at[24].append(("fb",))
    at[27].append(("ft",))
    at[34].append(("yt", 0))
    return at


PLAN = group_plan()
TRN = 7


def build_kernel(nc, x, wqT, wkT, wvT, woT, in_g, in_b, agg_w, agg_b, pn_g, pn_b, d1_w, d1_b, d2_w, d2_b,
                 bc_w, bc_b, gate_w, gate_b, out_g, out_b, rope_c, rope_s, pick, out):
    def dram(name, shape, dt):
        return nc.dram_tensor(name, shape, dt, kind="Internal").ap()

    xt_d = dram("xt_scratch", (B, 2, P, KT, T), F32)
    q_d = dram("q_scratch", (B * PAIRS, 3, 2, P, T), F32)
    k_d = dram("k_scratch", (B, 3, 2, P, T), F32)
    v_d = dram("v_scratch", (GROUPS, NT, P, VW), BF16)
    y_d = dram("y_scratch", (2, 1 + GROUPS, P, T), F32)

    with ExitStack() as outer:
        def osb(name, shape, dt):
            return outer.enter_context(nc.sbuf_tensor(name, shape, dt))

        ident = osb("ident", [P, P], F32)
        ident16 = osb("ident16", [P, P], BF16)
        mask_q = osb("mask_q", [P, P], BF16)
        mask_k = osb("mask_k", [P, P], BF16)
        mhalf = osb("mhalf", [P, 4], F32)

        project_phase(nc, x, wqT, wkT, wvT, rope_c, rope_s, xt_d, q_d, k_d, v_d,
                      ident, ident16, mask_q, mask_k, mhalf)
        bcast = osb("bcast", [P, B, D], F32)
        attention_phase(nc, x, in_g, in_b, agg_w, agg_b, pn_g, pn_b, d1_w, d1_b, d2_w, d2_b, bc_w, bc_b, pick,
                        q_d, k_d, v_d, y_d, ident, ident16, mask_q, mask_k, mhalf, bcast)
        output_phase(nc, x, woT, gate_w, gate_b, out_g, out_b, xt_d, y_d, mhalf, bcast, out)


def project_phase(nc, x, wqT, wkT, wvT, rope_c, rope_s, xt_d, q_d, k_d, v_d,
                  ident, ident16, mask_q, mask_k, mhalf):
    NB = 2 * B
    NP = PAIRS + 1
    QK = PAIRS * 256
    WN = QK + 256 + KV * HD
    with ExitStack() as ctx:
        def sb(name, shape, dt):
            return ctx.enter_context(nc.sbuf_tensor(name, shape, dt))

        def ps(name, shape, dt):
            return ctx.enter_context(nc.psum_tensor(name, shape, dt))

        def sem(name):
            return ctx.enter_context(nc.semaphore(name))

        w1 = sb("w1", [P, KT, WN], F32R)
        w2 = sb("w2", [P, KT, WN], F32R)
        xin = sb("xin", [P, 4, D], F32)
        xt = [[sb(f"xt{p}{i}", [P, KT, HALF], F32R) for i in range(2)] for p in range(2)]
        cs = sb("cs", [P, 2, T], F32)
        rt = sb("rt", [P, 4, HALF], F32)
        r1 = sb("r1", [P, 2, HALF], F32R)
        r2 = sb("r2", [P, 2, HALF], F32R)
        vp = sb("vp", [P, 2, KV, VW], BF16)
        vr = sb("vr", [P, KV, HD], F32)
        bst = sb("bst", [P, 4, 2, 6], F32)
        mv = sb("mv", [P, 4, 2], F32)
        ve = sb("ve", [P, 4], F32)
        rstd = sb("rstd", [P, 4], F32)
        tr = [ps(f"tr{i}", [P, HALF], F32) for i in range(2)]
        eo = [ps(f"eo{i}", [P, 2, HALF], F32) for i in range(2)]
        pv = [ps(f"pv{i}", [P, 512], F32) for i in range(2)]

        const_ready = sem("p_const")
        w_in, w1_done, w2_done = [sem(f"p_w_in{i}") for i in range(2)], sem("p_w1"), sem("p_w2")
        cs_in = sem("p_cs_in")
        x_in, stats_done, rstd_done, xn_done = sem("p_x_in"), sem("p_stats"), sem("p_rstd"), sem("p_xn")
        stat_link, issue = sem("p_link"), sem("p_issue")
        tr_done, x1_done, x2_done = sem("p_tr"), sem("p_x1"), sem("p_x2")
        xt_out = [sem(f"p_xt_out{i}") for i in range(2)]
        pair_done, mul_done, rope_done = sem("p_pair"), sem("p_mul"), sem("p_rope")
        r1_done, r2_done, r_out = sem("p_r1"), sem("p_r2"), sem("p_r_out")
        v_done, v1_done, vr_done, v2_done, v3_done = (sem(f"p_v{i}") for i in "abcde")
        v_out = [sem(f"p_v_out{i}") for i in range(2)]
        block = ctx.enter_context(nc.Block())

        wst = [v[:].rearrange("p a t -> p (a t)")[:, 0:WN] for v in (rt, cs)]
        srcs = [(wqT, 0, QK), (wkT, QK, 256), (wvT, QK + 256, KV * HD)]

        def x_block(n):
            return x[bass.ds(n * HALF, HALF)].rearrange("(t p) d -> p t d", p=P)

        @block.sync
        def _(sp):
            sp.dma_start(xin[:], x_block(0)).then_inc(x_in, 16)
            for k in range(KT):
                for src, c0, w in srcs:
                    sp.dma_start(wst[k % 2][:, c0:c0 + w], src[k * P:(k + 1) * P, :]).then_inc(w_in[k % 2], 16)
                if k >= 1:
                    sp.wait_ge(w2_done, k)
            sp.wait_ge(w2_done, KT)
            sp.dma_start(cs[:, 0, :], rope_c).then_inc(cs_in, 16)
            sp.dma_start(cs[:, 1, :], rope_s).then_inc(cs_in, 16)
            sp.wait_ge(tr_done, KT)
            sp.dma_start(xin[:], x_block(1)).then_inc(x_in, 16)
            with sp.Fori(0, B) as b:
                for half in range(2):
                    n = 2 * b + half
                    sp.wait_ge(x2_done, KT * n + KT)
                    for p in range(2):
                        sp.dma_start(xt_d[bass.ds(b, 1), p, :, :, half * HALF:(half + 1) * HALF]
                                     .rearrange("a p k t -> (a p) k t"), f32(xt[p][half][:])).then_inc(xt_out[half], 16)
                    for q in range(NP):
                        sp.wait_ge(r2_done, NP * n + q + 2)
                        dst, blk, parts = (q_d, b * PAIRS + q, (r1, r1, r2)) if q < PAIRS else (k_d, b, (r1, r2, r1))
                        for part, r in enumerate(parts):
                            sp.dma_start(dst[bass.ds(blk, 1), part, :, :, half * HALF:(half + 1) * HALF]
                                         .rearrange("a e p t -> (a p) e t"), f32(r[:])).then_inc(r_out, 16)
                    sp.wait_ge(tr_done, KT * n + 2 * KT)
                    sp.dma_start(xin[:], x_block((n + 2) % NB)).then_inc(x_in, 16)
                    for t in range(4):
                        sp.wait_ge(v3_done, 4 * n + t + 2)
                        sp.dma_start(v_d[bass.ds(b * KV, KV), half * 4 + t].rearrange("g p c -> p g c"),
                                     vp[:, t % 2]).then_inc(v_out[t % 2], 16)
            sp.wait_ge(x_in, 16 * (NB + 2))
            for i in range(2):
                sp.wait_ge(xt_out[i], 32 * B + 1)
                sp.wait_ge(v_out[i], 32 * NB + 1)
            sp.wait_ge(r_out, 48 * NP * NB + 1)

        @block.gpsimd
        def _(pool):
            nc.gpsimd.memset(mhalf[:], -0.5).then_inc(const_ready, 1)
            nc.gpsimd.memset(ident[:], 0.0).then_inc(const_ready, 1)
            nc.gpsimd.memset(mask_q[:], 0.0).then_inc(const_ready, 1)
            nc.gpsimd.memset(mask_k[:], 0.0).then_inc(const_ready, 1)
            nc.gpsimd.memset(vp[:], 0.0).then_inc(const_ready, 1)
            pool.wait_ge(const_ready, 5)
            nc.gpsimd.memset(vp[:, :, :, 0:1], 1.0).then_inc(const_ready, 1)
            nc.gpsimd.affine_select(out=ident[:], in_=ident[:], compare_op=ALU.not_equal, fill=1.0, base=0,
                                    pattern=[[-1, P]], channel_multiplier=1).then_inc(const_ready, 1)
            nc.gpsimd.affine_select(out=mask_q[:], in_=mask_q[:], compare_op=ALU.is_ge, fill=NEG, base=0,
                                    pattern=[[-1, P]], channel_multiplier=1).then_inc(const_ready, 1)
            nc.gpsimd.affine_select(out=mask_k[:], in_=mask_k[:], compare_op=ALU.is_ge, fill=NEG, base=0,
                                    pattern=[[1, P]], channel_multiplier=-1).then_inc(const_ready, 1)
            pool.wait_ge(const_ready, 9)
            nc.gpsimd.tensor_copy(ident16[:], ident[:]).then_inc(const_ready, 1)

            def rstd_of(n):
                pool.wait_ge(stats_done, n + 1)
                nc.gpsimd.tensor_tensor(rstd[:], ve[:], mhalf[:], ALU.pow).then_inc(rstd_done, 1)

            rstd_of(0)
            with pool.Fori(0, B) as b:
                for half in range(2):
                    n = 2 * b + half
                    rstd_of(n + 1)
                    for q in range(NP):
                        pool.wait_ge(r1_done, NP * n + q + 1)
                        nc.gpsimd.tensor_tensor(r2[:], rt[:, 0:2, :], f32(r1[:]), ALU.subtract).then_inc(r2_done, 1)
                    for t in range(4):
                        pool.wait_ge(v2_done, 4 * n + t + 1)
                        nc.gpsimd.tensor_tensor(vp[:, t % 2, :, 65:97], vr[:], vp[:, t % 2, :, 33:65],
                                                ALU.subtract).then_inc(v3_done, 1)

        @block.scalar
        def _(act):
            act.wait_ge(const_ready, 6)
            def round_x(m, par, k):
                act.wait_ge(tr_done, KT * m + k + 1)
                nc.scalar.activation(xt[0][par][:, k, :], tr[k % 2][:], ACT.Copy).then_inc(x1_done, 1)

            for k in range(KT):
                act.wait_ge(w_in[k % 2], 48 * (k // 2 + 1))
                nc.scalar.activation(w1[:, k, :], wst[k % 2], ACT.Copy).then_inc(w1_done, 1)
                round_x(0, 0, k)
            with act.Fori(0, B) as b:
                for half in range(2):
                    n = 2 * b + half
                    for q in range(NP):
                        act.wait_ge(rope_done, NP * n + q + 1)
                        act.wait_ge(r_out, 48 * (NP * n + q) + 1)
                        nc.scalar.activation(r1[:], rt[:, 0:2, :], ACT.Copy).then_inc(r1_done, 1)
                        for k in X_TR[q]:
                            if k == 0 and half == 0:
                                act.wait_ge(xt_out[1], 32 * b + 1)
                            elif k == 0:
                                act.wait_ge(xt_out[0], 32 * b + 33)
                            round_x(n + 1, 1 - half, k)
                    for t in range(4):
                        act.wait_ge(v_done, 4 * n + t + 1)
                        act.wait_ge(v_out[t % 2], 16 * (2 * n + t // 2) + 1)
                        nc.scalar.activation(vp[:, t % 2, :, 1:33], pv[t % 2][:, 0:KV * HD]
                                             .rearrange("p (g d) -> p g d", g=KV), ACT.Copy).then_inc(v1_done, 1)
                        act.wait_ge(vr_done, 4 * n + t + 3)
                        nc.scalar.activation(vp[:, t % 2, :, 33:65], vr[:], ACT.Copy).then_inc(v2_done, 1)

        @block.vector
        def _(dve):
            for w, v in ((r_out, 1), (xt_out[0], 1), (xt_out[1], 1), (v_out[0], 1), (v_out[1], 1), (r2_done, 1),
                         (v3_done, 1), (mul_done, 2), (vr_done, 2)):
                dve.sem_inc(w, v)

            def normalise(m):
                dve.wait_ge(x_in, 16 * (m + 1))
                for t in range(4):
                    for c in range(2):
                        last = nc.vector.bn_stats(bst[:, t, c, :], xin[:, t, c * 512:(c + 1) * 512])
                last.then_inc(stat_link, 1)
                dve.wait_ge(stat_link, 2 * m + 1)
                dve.sem_inc(issue, 1)
                for t in range(4):
                    last = nc.vector.bn_aggr(mv[:, t, :], bst[:, t].rearrange("p a b -> p (a b)"))
                last.then_inc(stat_link, 1)
                dve.wait_ge(stat_link, 2 * m + 2)
                nc.vector.tensor_scalar(ve[:], mv[:, :, 1], EPS_X, None, ALU.add).then_inc(stats_done, 1)
                dve.wait_ge(rstd_done, m + 1)
                for t in range(4):
                    nc.vector.tensor_scalar(xin[:, t, :], xin[:, t, :], mv[:, t, 0:1], rstd[:, t:t + 1],
                                            ALU.subtract, ALU.mult).then_inc(xn_done, 1)

            def rest_x(m, par, k):
                dve.wait_ge(x1_done, KT * m + k + 1)
                nc.vector.tensor_tensor(xt[1][par][:, k, :], tr[k % 2][:], f32(xt[0][par][:, k, :]),
                                        ALU.subtract).then_inc(x2_done, 1)

            normalise(0)
            for k in range(KT):
                dve.wait_ge(w1_done, k + 1)
                nc.vector.tensor_tensor(w2[:, k, :], wst[k % 2], f32(w1[:, k, :]), ALU.subtract).then_inc(w2_done, 1)
                rest_x(0, 0, k)
            dve.wait_ge(cs_in, 32)
            with dve.Fori(0, B) as b:
                for half in range(2):
                    n = 2 * b + half
                    tok = slice(half * HALF, (half + 1) * HALF)
                    for q in range(NP):
                        bank = eo[(half + q) % 2]
                        dve.wait_ge(pair_done, NP * n + q + 1)
                        dve.wait_ge(r2_done, NP * n + q + 1)
                        for o, e, s in ((0, 0, 0), (1, 0, 1), (2, 1, 1), (3, 1, 0)):
                            last = nc.vector.tensor_tensor(rt[:, o, :], bank[:, e, :], cs[:, s, tok], ALU.mult)
                        last.then_inc(mul_done, 1)
                        dve.wait_ge(mul_done, NP * n + q + 3)
                        nc.vector.tensor_tensor(rt[:, 0, :], rt[:, 0, :], rt[:, 2, :], ALU.subtract)
                        nc.vector.tensor_tensor(rt[:, 1, :], rt[:, 1, :], rt[:, 3, :], ALU.add).then_inc(rope_done, 1)
                        if q == 0:
                            normalise(n + 1)
                        for k in X_TR[q]:
                            rest_x(n + 1, 1 - half, k)
                    for t in range(4):
                        dve.wait_ge(v1_done, 4 * n + t + 1)
                        dve.wait_ge(v3_done, 4 * n + t + 1)
                        nc.vector.tensor_tensor(vr[:], pv[t % 2][:, 0:KV * HD].rearrange("p (g d) -> p g d", g=KV),
                                                vp[:, t % 2, :, 1:33], ALU.subtract).then_inc(vr_done, 1)

        @block.tensor
        def _(pe):
            def transpose_x(m, k, first=False):
                if k == 0:
                    pe.wait_ge(xn_done, 4 * m + 4)
                if not (first and k < 2):
                    pe.wait_ge(x2_done, KT * m + k - 1)
                for t in range(4):
                    last = nc.tensor.transpose(tr[k % 2][:, t * P:(t + 1) * P], xin[:, t, k * P:(k + 1) * P], ident[:])
                last.then_inc(tr_done, 1)

            def product(out, lhs, rhs):
                parts = [(0, 0), (0, 1), (1, 0)]
                for k in range(KT):
                    for a, c in parts:
                        last = nc.tensor.matmul(out, lhs[a](k), rhs[c](k), start=(k == 0 and (a, c) == (0, 0)),
                                                stop=(k == KT - 1 and (a, c) == (1, 0)))
                return last

            ws = (w1, w2)
            pe.wait_ge(const_ready, 10)
            for k in range(KT):
                transpose_x(0, k, first=True)
            pe.wait_ge(w2_done, KT)
            with pe.Fori(0, B) as b:
                for half in range(2):
                    n = 2 * b + half
                    xs = [lambda k, p=p: xt[p][half][:, k, :] for p in range(2)]
                    pe.wait_ge(x2_done, KT * n + KT)
                    for q in range(NP):
                        bank = eo[(half + q) % 2]
                        pe.wait_ge(mul_done, NP * n + q + 1)
                        for e in range(2):
                            c0 = q * 256 + e * P
                            last = product(bank[:, e, :], [lambda k, w=w: w[:, k, c0:c0 + P] for w in ws], xs)
                        last.then_inc(pair_done, 1)
                        for k in X_TR[q]:
                            transpose_x(n + 1, k)
                    for t in range(4):
                        pe.wait_ge(vr_done, 4 * n + t + 1)
                        last = product(pv[t % 2][:, 0:KV * HD],
                                       [lambda k, p=p: xt[p][half][:, k, t * P:(t + 1) * P] for p in range(2)],
                                       [lambda k, w=w: w[:, k, QK + 256:WN] for w in ws])
                        last.then_inc(v_done, 1)


X_TR = [[], [], [0, 1, 2], [3, 4, 5], [6, 7]]


def attention_phase(nc, x, in_g, in_b, agg_w, agg_b, pn_g, pn_b, d1_w, d1_b, d2_w, d2_b, bc_w, bc_b, pick,
                    q_d, k_d, v_d, y_d, ident, ident16, mask_q, mask_k, mhalf, bcast):
    QR = 3 * HD
    with ExitStack() as ctx:
        def sb(name, shape, dt):
            return ctx.enter_context(nc.sbuf_tensor(name, shape, dt))

        def ps(name, shape, dt):
            return ctx.enter_context(nc.psum_tensor(name, shape, dt))

        def sem(name):
            return ctx.enter_context(nc.semaphore(name))

        qs = [sb(f"qs{i}", [QR + 1, REP, T], F32R) for i in range(2)]
        ks = [sb(f"ks{i}", [QR + 1, T], F32R) for i in range(2)]
        vs = [sb(f"vs{i}", [P, NT, VW], BF16) for i in range(2)]
        p1 = [sb(f"p1_{i}", [P, REP, PROB_W[i]], F16) for i in range(2)]
        p2 = [sb(f"p2_{i}", [P, REP, PROB_W[i]], F16) for i in range(2)]
        pf = sb("pf", [P, 4, HALF], F32)
        mx = [sb(f"mx{i}", [P, NT, REP], F32) for i in range(2)]
        mt = [sb(f"mt{i}", [REP, HALF], F32R) for i in range(2)]
        rinv = sb("rinv", [P, REP], F32)
        yv = sb("yv", [P, REP, HD], F32)
        yn = sb("yn", [P, 2, 4, P], F32)
        y1 = [sb(f"y1_{i}", [P, HALF], F32R) for i in range(2)]
        y2 = [sb(f"y2_{i}", [P, HALF], F32R) for i in range(2)]
        wch = [sb(f"wch{i}", [P, 4, D], F32) for i in range(2)]
        fsb = sb("fsb", [P, HALF], F32)
        fr = sb("fr", [P, KT, B], F32)
        hpre = sb("hpre", [P, KT, B], F32)
        b1c = sb("b1c", [P, KT], F32)
        t_in = sb("t_in", [P, KT, 32], F32)
        h_in = sb("h_in", [P, KT, 32], F32)
        th = sb("th", [P, KT, B], F32)
        cen = sb("cen", [P, KT, B], F32)
        sq = sb("sq", [P, KT, B], F32)
        s1 = sb("s1", [P, B], F32)
        s2 = sb("s2", [P, B], F32)
        ve = sb("f_ve", [P, B], F32)
        rs = sb("f_rs", [P, B], F32)
        onesd = sb("onesd", [P, P], F32)
        fvec = sb("fvec", [P, 4, KT], F32)
        fbias = sb("fbias", [P, HALF], F32)
        picks = sb("picks", [P, 2 * B, P], F32)
        lst = sb("lst", [B, 2, 6], F32)
        lmv = sb("lmv", [B, 2], F32)
        lve = sb("lve", [B, 1], F32)
        lrs = sb("lrs", [B, 1], F32)
        xl = pf[0:B, 0:2, :].rearrange("p a b -> p (a b)")
        gl = pf[0:B, 2:4, :].rearrange("p a b -> p (a b)")
        bl = yn[0:B].rearrange("p a b c -> p (a b c)")

        mxp = [ps(f"mxp{i}", [P, 2 * HALF], F32) for i in range(2)]
        stp = [ps(f"stp{i}", [P, HALF], F32) for i in range(2)]
        pvp = ps("pvp", [P, 512], F32)
        trp = ps("trp", [P, 512], F32)

        qk_in = [sem(f"a_qk_in{i}") for i in range(2)]
        v_in = [sem(f"a_v_in{i}") for i in range(2)]
        m_in = [sem(f"a_m_in{i}") for i in range(4)]
        w_in = [sem(f"a_w_in{i}") for i in range(2)]
        y_out = [sem(f"a_y_out{i}") for i in range(2)]
        b1_in, c_in = sem("a_b1_in"), sem("a_c_in")
        xl_in, gb_in = sem("a_xl_in"), sem("a_gb_in")
        issue = sem("a_issue")
        init, init_p = sem("a_init"), sem("a_init_p")
        st_done, act_done, sub_done = sem("a_st"), sem("a_act"), sem("a_sub")
        mx_done, mx_free = sem("a_mx"), sem("a_mx_free")
        pv_done, pv_free = sem("a_pv"), sem("a_pv_free")
        tr_full, tr_free, y1_done = sem("a_tr_full"), sem("a_tr_free"), sem("a_y1")
        hp_done, h_done, t_done = sem("a_hp"), sem("a_h"), sem("a_t")
        ln_sum, ln_ve, ln_rs = sem("a_ln_sum"), sem("a_ln_ve"), sem("a_ln_rs")
        link_s = sem("a_link")
        l_ve, l_rs = sem("a_l_ve"), sem("a_l_rs")
        block = ctx.enter_context(nc.Block())

        TR0 = 7
        TR_STEP = NT * TRN + 2

        def trb(s, c, par):
            return TR0 + s * TR_STEP + (2 * c + par) * TRN

        ORDER = [e for slot in PLAN for e in slot if e[0] in ("mt", "fa", "fb", "ft", "yt")]
        use = {e: r for r, e in enumerate(ORDER)}
        PV_IDX = {i: i - 4 if i >= 4 else i + 4 for i in range(NT)}
        LAST = TR0 + STEPS * TR_STEP

        @block.sync
        def _(sp):
            def load_v(par, m):
                sp.dma_start(vs[par][:], v_d[bass.ds(m, 1)].rearrange("a t p c -> p (a t) c")).then_inc(v_in[par], 16)

            def load_w(burst, src):
                for kh in range(2):
                    sp.dma_start(wch[burst][:, 2 * kh:2 * kh + 2, :], src(kh * 512 + burst * 256)
                                 .rearrange("(k p) n -> p k n", p=P)).then_inc(w_in[burst], 16)

            def whole(w):
                return lambda r: w[r:r + 256, :]

            def d1_chunk(c):
                return lambda r: d1_w[r:r + 256, bass.ds(c * D, D)]

            def d2_chunk(c):
                return lambda r: d2_w[bass.ds(c * D + r, 256), :]

            def store_y(half, slot):
                for part, y in enumerate((y1, y2)):
                    sp.dma_start(y_d[part, bass.ds(slot, 1), :, half * HALF:(half + 1) * HALF]
                                 .rearrange("a p t -> (a p) t"), f32(y[half][:])).then_inc(y_out[half], 16)

            xlast = x.rearrange("(b t) d -> b t d", b=B)[:, T - 1, :]
            sp.dma_start(xl, xlast).then_inc(xl_in, 16)
            for r in range(B):
                sp.dma_start(gl[r:r + 1, :], in_g).then_inc(gb_in, 16)
                sp.dma_start(bl[r:r + 1, :], in_b).then_inc(gb_in, 16)
            load_v(0, 0)
            for r, v in enumerate((agg_b, pn_g, pn_b, d2_b)):
                sp.dma_start(fvec[:, r, :], v).then_inc(c_in, 16)
            sp.dma_start(picks[:], pick).then_inc(c_in, 16)
            sp.dma_start(b1c[:], d1_b[0]).then_inc(b1_in, 16)
            load_w(0, whole(agg_w))
            load_w(1, whole(agg_w))
            sp.wait_ge(init, 1)
            for nb in range(2):
                for r in range(B):
                    sp.dma_start(fbias[64 * nb + r:64 * nb + r + 1, :], bc_b[:, nb * HALF:(nb + 1) * HALF]).then_inc(c_in, 16)
            sp.wait_ge(tr_full, 3)
            load_w(0, d1_chunk(0))
            sp.wait_ge(tr_full, 4)
            load_w(1, d1_chunk(0))
            with sp.Fori(0, STEPS) as s:
                with sp.Fori(0, CH) as c:
                    for par in range(2):
                        it = s * CH + c
                        n = it * 2 + par
                        nxt = 1 - par
                        tb = trb(s, c, par)
                        sp.wait_ge(tr_full, tb + use[("fa",)] + 1)
                        cn = (c + par) % CH
                        load_w(0, d2_chunk(c) if par == 0 else d1_chunk(cn))
                        sp.wait_ge(pv_done, NT * n + 4 + 1)
                        load_v(nxt, (n + 1) % GROUPS)
                        sp.wait_ge(tr_free, tb + use[("yt", 1)] + 2)
                        store_y(1, n)
                        sp.wait_ge(tr_full, tb + use[("fb",)] + 1)
                        load_w(1, d2_chunk(c) if par == 0 else d1_chunk(cn))
                        if par == 1:
                            sp.wait_ge(hp_done, it + 1)
                            sp.dma_start(b1c[:], d1_b[bass.ds(cn, 1)].rearrange("a p k -> (a p) k")).then_inc(b1_in, 16)
                        sp.wait_ge(tr_free, tb + use[("yt", 0)] + 2)
                        store_y(0, n + 1)
            for burst in range(2):
                sp.wait_ge(w_in[burst], 32 * (GROUPS + 2))
                load_w(burst, whole(bc_w))
            sp.wait_ge(tr_free, LAST + 1 + 1)
            store_y(1, GROUPS)
            for half in range(2):
                sp.wait_ge(y_out[half], 32 * (GROUPS + 1 - (1 - half)) + 1)
            for par in range(2):
                sp.wait_ge(v_in[par], 16 * (GROUPS // 2 + (1 - par)))
                sp.wait_ge(w_in[par], 32 * (GROUPS + 3))
            sp.wait_ge(b1_in, 16 * (GROUPS // 2 + 1))

        @block.gpsimd
        def _(pool):
            def load_qk(par, blk, m):
                pool.sem_inc(issue, 1)
                nc.gpsimd.dma_start(qs[par][0:QR].rearrange("p h t -> p (h t)"),
                                    q_d[bass.ds(blk, 1)].rearrange("a r e (f g) t -> (a r e f) (g t)", g=2 * REP)
                                    [:, par * REP * T:(par + 1) * REP * T]).then_inc(qk_in[par], 16)
                nc.gpsimd.dma_start(ks[par][0:QR], k_d[bass.ds(m // KV, 1)]
                                    .rearrange("a r e (f g) t -> (a r e f) g t", g=KV)[:, bass.ds(m % KV, 1), :]
                                    .rearrange("p g t -> p (g t)")).then_inc(qk_in[par], 16)

            def move_mt(half, par):
                pool.sem_inc(issue, 1)
                nc.gpsimd.dma_start(qs[par][QR:QR + 1, :, half * HALF:(half + 1) * HALF],
                                    f32(mt[half][:])).then_inc(m_in[2 * half + par], 16)

            load_qk(0, 0, 0)
            nc.gpsimd.memset(fbias[:], 0.0).then_inc(init, 1)
            for t in (t_in, h_in):
                nc.gpsimd.memset(t[:], 0.0).then_inc(init, 1)
            nc.gpsimd.memset(onesd[:], 1.0 / D).then_inc(init, 1)
            for i in range(2):
                pool.wait_ge(init, 4 + i)
                nc.gpsimd.memset(f32(ks[i][QR:QR + 1, :]), 1.0).then_inc(init, 1)
            pool.wait_ge(init, 6)
            nc.gpsimd.memset(vs[1][:], 1.0).then_inc(init, 1)
            for k in range(2):
                pool.wait_ge(l_ve, k + 1)
                nc.gpsimd.tensor_tensor(lrs[:], lve[:], mhalf[0:B, 0:1], ALU.pow).then_inc(l_rs, 1)

            def ln_pool(k):
                pool.wait_ge(ln_ve, k + 1)
                nc.gpsimd.tensor_tensor(rs[:], ve[:], mhalf[:], ALU.pow).then_inc(ln_rs, 1)

            nc.gpsimd.memset(p2[1][:], 1.0).then_inc(init_p, 1)
            pool.wait_ge(tr_free, 3)
            move_mt(0, 0)
            ln_pool(0)
            with pool.Fori(0, STEPS) as s:
                with pool.Fori(0, CH) as c:
                    for par in range(2):
                        it = s * CH + c
                        n = it * 2 + par
                        tb = trb(s, c, par)
                        for u, (half, h, (_, _, (c0, c1), at)) in enumerate(ST):
                            w = c1 - c0
                            if u == MT1_OUT:
                                pool.wait_ge(tr_free, tb + use[("mt", 1)] + 2)
                                move_mt(1, par)
                            if u == MT0_OUT:
                                pool.wait_ge(tr_free, tb + use[("mt", 0)] + 2)
                                move_mt(0, 1 - par)
                            pool.wait_ge(act_done, NST * n + u + 3)
                            nc.gpsimd.tensor_tensor(p2[half][:, h, at:at + w], pf[:, u % 4, 0:w],
                                                    p1[half][:, h, at:at + w], ALU.subtract).then_inc(sub_done, 1)
                            if u == 0:
                                load_qk(1 - par, it if par == 0 else (it + 1) % (GROUPS // 2), (n + 1) % GROUPS)
                ln_pool(s + 1)
            for par in range(2):
                pool.wait_ge(qk_in[par], 32 * (GROUPS // 2 + (1 - par)))
            pool.wait_ge(m_in[0], 16 * (GROUPS // 2 + 1))

        @block.scalar
        def _(act):
            def copy_burst(tu):
                act.wait_ge(tr_full, tu + 1)
                nc.scalar.activation(fsb[:], trp[:], ACT.Copy).then_inc(tr_free, 1)

            def round_y(half, tu, n, k):
                act.wait_ge(tr_full, tu + 1)
                act.wait_ge(y_out[half], n * 32 + 1)
                nc.scalar.activation(y1[half][:], trp[:], ACT.Copy).then_inc(y1_done, 1)

            copy_burst(2)
            with act.Fori(0, STEPS) as s:
                with act.Fori(0, CH) as c:
                    for par in range(2):
                        it = s * CH + c
                        n = it * 2 + par
                        tb = trb(s, c, par)
                        for u, (half, h, (_, _, (c0, c1), at)) in enumerate(ST):
                            w = c1 - c0
                            act.wait_ge(st_done, NST * n + u + 2)
                            if u == 0:
                                act.wait_ge(pv_done, NT * n + 1)
                            if u == HALF_ST:
                                act.wait_ge(pv_done, NT * n + 4 + 1)
                            nc.scalar.activation(p1[half][:, h, at:at + w], stp[u % 2][:, c0:c1], ACT.Exp, scale=SCALE)
                            act.wait_ge(sub_done, NST * n + u + 1)
                            nc.scalar.activation(pf[:, u % 4, 0:w], stp[u % 2][:, c0:c1], ACT.Exp,
                                                 scale=SCALE).then_inc(act_done, 1)
                            for e in (PLAN[u - 1] if u else []):
                                if e == ("fa",):
                                    copy_burst(tb + use[e])
                                elif e[0] == "yt":
                                    round_y(e[1], tb + use[e], n, None)
                                elif e == ("ft",) and par == 0:
                                    act.wait_ge(hp_done, it + 1)
                                    nc.scalar.activation(h_in[:, :, 0:B], hpre[:], ACT.Gelu).then_inc(h_done, 1)
            round_y(1, LAST, GROUPS, None)
            copy_burst(LAST + 1)

        @block.vector
        def _(dve):
            links = {"n": 0}

            def link(ins, base):
                links["n"] += 1
                ins.then_inc(link_s, 1)
                dve.wait_ge(link_s, base + links["n"])

            def bc(ap, n):
                return ap.unsqueeze(2).to_broadcast([ap.shape[0], ap.shape[1], n])

            def rows(ap):
                return ap.unsqueeze(1).to_broadcast([P, KT, B])

            def layernorm(tu, k, base):
                nc.vector.tensor_reduce(s1[:], th[:].rearrange("p k r -> p r k"), AX.X, ALU.add).then_inc(ln_sum, 1)
                dve.wait_ge(tr_full, tu + 1)
                nc.vector.tensor_tensor(cen[:], th[:], rows(trp[:, 0:B]), ALU.subtract).then_inc(tr_free, 1)
                dve.wait_ge(tr_free, tu + 2)
                link(nc.vector.tensor_tensor(sq[:], cen[:], cen[:], ALU.mult), base)
                nc.vector.tensor_reduce(s2[:], sq[:].rearrange("p k r -> p r k"), AX.X, ALU.add).then_inc(ln_sum, 1)
                dve.wait_ge(tr_full, tu + 2)
                nc.vector.tensor_scalar(ve[:], trp[:, 0:B], EPS_F, None, ALU.add).then_inc(ln_ve, 1)
                dve.wait_ge(ln_rs, k + 1)
                nc.vector.tensor_tensor(cen[:], cen[:], rows(rs[:]), ALU.mult).then_inc(tr_free, 1)
                dve.wait_ge(tr_free, tu + 3)
                link(nc.vector.tensor_tensor(cen[:], cen[:], bc(fvec[:, 1, :], B), ALU.mult), base)
                nc.vector.tensor_tensor(t_in[:, :, 0:B], cen[:], bc(fvec[:, 2, :], B), ALU.add).then_inc(t_done, 1)

            def row_max(k, count, par):
                i, h, per = MX[k]
                dve.wait_ge(mx_done, count + 1)
                bank, w = mxp[k % 2], (i + 1) * P
                src = bank[:].rearrange("p (h s) -> p h s", h=per)[:, :, 0:w]
                nc.vector.tensor_reduce(mx[par][:, i, h:h + per], src, AX.X, ALU.max, negate=True).then_inc(mx_free, 1)

            def max_rows(half, tu):
                dve.wait_ge(tr_full, tu + 1)
                nc.vector.tensor_scalar(mt[half][:], trp[0:REP, :], LIFT, None, ALU.add).then_inc(tr_free, 1)

            def add_burst(tu):
                dve.wait_ge(tr_full, tu + 1)
                nc.vector.tensor_tensor(fsb[:], trp[:], fsb[:], ALU.add).then_inc(tr_free, 1)

            def chunk_out(tu, base):
                dve.wait_ge(tr_full, tu + 1)
                v = trp[:].rearrange("p (c n k r) -> p n c r k", c=4, n=2, k=2)
                for nb in range(2):
                    last = nc.vector.tensor_reduce(fr[:, 4 * nb:4 * nb + 4, :], v[:, nb, :, 0:B, :], AX.X, ALU.add)
                last.then_inc(tr_free, 1)
                dve.wait_ge(tr_free, tu + 2)

            def normalise(i, count, base):
                dve.wait_ge(pv_done, count + 2)
                v = pvp[:, 0:REP * VW].rearrange("p (h c) -> p h c", c=VW)
                nc.vector.reciprocal(rinv[:], v[:, :, 0])
                link(nc.vector.tensor_reduce(yv[:], v[:, :, 1:1 + 3 * HD].rearrange("p h (t d) -> p h d t", t=3),
                                             AX.X, ALU.add), base)
                nc.vector.tensor_tensor(yn[:, i // 4, i % 4, :].rearrange("p (h d) -> p h d", h=REP), yv[:],
                                        bc(rinv[:], HD), ALU.mult).then_inc(pv_free, 1)
                dve.wait_ge(pv_free, count + 2)

            def rest_y(half, tu, k):
                dve.wait_ge(y1_done, k + 1)
                nc.vector.tensor_tensor(y2[half][:], trp[:], f32(y1[half][:]), ALU.subtract).then_inc(tr_free, 1)

            for w, v in (((st_done, 1), (pv_done, 1), (pv_free, 1), (tr_free, 1), (act_done, 2),
                                        (sub_done, 4), (y_out[0], 1), (y_out[1], 1))):
                dve.sem_inc(w, v)
            nc.vector.memset(p1[1][:], 1.0).then_inc(init_p, 1)

            dve.wait_ge(xl_in, 16)
            for k, eps in enumerate((EPS_X, EPS_F)):
                for cc in range(2):
                    last = nc.vector.bn_stats(lst[:, cc, :], xl[:, cc * 512:(cc + 1) * 512])
                link(last, 0)
                link(nc.vector.bn_aggr(lmv[:], lst[:].rearrange("p a b -> p (a b)")), 0)
                nc.vector.tensor_scalar(lve[:], lmv[:, 1:2], eps, None, ALU.add).then_inc(l_ve, 1)
                dve.wait_ge(l_rs, k + 1)
                link(nc.vector.tensor_scalar(xl, xl, lmv[:, 0:1], lrs[:], ALU.subtract, ALU.mult), 0)
            dve.wait_ge(gb_in, 128)
            link(nc.vector.tensor_tensor(xl, xl, gl, ALU.mult), 0)
            nc.vector.tensor_tensor(xl, xl, bl, ALU.add).then_inc(t_done, 1)
            dve.wait_ge(tr_full, 1)
            dve.wait_ge(init, 4)
            nc.vector.tensor_copy(t_in[:, :, 0:B], trp[:, 0:KT * B].rearrange("p (k r) -> p k r", r=B)).then_inc(tr_free, 1)
            for k in range(NMX):
                row_max(k, k, 0)
            max_rows(0, 1)
            add_burst(3)
            chunk_out(4, 0)
            dve.wait_ge(c_in, 16 * 13)
            link(nc.vector.tensor_tensor(th[:], fr[:], bc(fvec[:, 0, :], B), ALU.add), 0)
            layernorm(5, 0, 0)
            BASE = links["n"]
            with dve.Fori(0, STEPS) as s:
                with dve.Fori(0, CH) as c:
                    links["n"] = 0
                    it = s * CH + c
                    base = it * LINKS_TURN + s * LINKS_STEP + BASE
                    for par in range(2):
                        n = it * 2 + par
                        tb = trb(s, c, par)
                        for slot in PLAN:
                            for e in slot:
                                if e[0] == "mx":
                                    row_max(e[1], (n + 1) * NMX + e[1], 1 - par)
                                elif e[0] == "pv" and e[3] == REP - 1:
                                    normalise(e[2], n * NT + PV_IDX[e[2]], base)
                                elif e[0] == "mt":
                                    half, tp = e[1], par if e[1] == 1 else 1 - par
                                    if half == 0:
                                        dve.wait_ge(m_in[par], (it + 1) * 16)
                                    elif par == 1:
                                        dve.wait_ge(m_in[2], (it + 1) * 16)
                                    else:
                                        dve.wait_ge(st_done, n * NST + 1)
                                    max_rows(half, tb + use[e])
                                elif e[0] == "fb":
                                    add_burst(tb + use[e])
                                elif e[0] == "ft":
                                    chunk_out(tb + use[e], base)
                                    if par == 0:
                                        dve.wait_ge(b1_in, (it + 1) * 16)
                                        nc.vector.tensor_tensor(hpre[:], fr[:], bc(b1c[:], B), ALU.add).then_inc(hp_done, 1)
                                    else:
                                        link(nc.vector.tensor_tensor(th[:], th[:], fr[:], ALU.add), base)
                                elif e[0] == "yt":
                                    rest_y(e[1], tb + use[e], n * 2 + (0 if e[1] == 1 else 1))
                    assert links["n"] == LINKS_TURN, links["n"]
                links["n"] = 0
                base = (s + 1) * (CH * LINKS_TURN) + s * LINKS_STEP + BASE
                link(nc.vector.tensor_tensor(th[:], th[:], bc(fvec[:, 3, :], B), ALU.add), base)
                layernorm(TR0 + s * TR_STEP + NT * TRN, s + 1, base)
                assert links["n"] == LINKS_STEP, links["n"]
            base = BASE + STEPS * (CH * LINKS_TURN + LINKS_STEP)
            links["n"] = 0
            for i in range(4, NT):
                normalise(i, GROUPS * NT + i - 4, base)
            rest_y(1, LAST, 2 * GROUPS)
            nc.vector.tensor_copy(h_in[:, :, 0:B], th[:]).then_inc(t_done, 1)
            add_burst(LAST + 2)
            dve.wait_ge(tr_free, LAST + 4)
            nc.vector.tensor_tensor(fsb[:], fsb[:], fbias[:], ALU.add).then_inc(t_done, 1)
            for k in range(2 * B):
                dve.wait_ge(tr_full, LAST + 4 + k)
                nc.vector.tensor_copy(bcast[:, k // 2, (k % 2) * HALF:(k % 2 + 1) * HALF], trp[:]).then_inc(tr_free, 1)

        @block.tensor
        def _(pe):
            def scores_max(k, count, par, first=False):
                i, h0, per = MX[k]
                if not first:
                    pe.wait_ge(mx_free, count - 1)
                bank, step = mxp[k % 2], 2 * HALF // per
                for hh in range(per):
                    lhs = qs[par][0:QR, h0 + hh, i * P:(i + 1) * P]
                    if per == 1:
                        nc.tensor.matmul(bank[:, 0:512], lhs, ks[par][0:QR, 0:512], start=True, stop=True)
                        w = [256, 256, 384, 512][i - 4]
                        nc.tensor.matmul(bank[:, 512:512 + w], lhs, ks[par][0:QR, 512:512 + w], start=True, stop=False)
                    else:
                        w = [256, 256, 384, 512][i]
                        nc.tensor.matmul(bank[:, hh * step:hh * step + w], lhs, ks[par][0:QR, 0:w], start=True, stop=False)
                    at = hh * step + i * P
                    last = nc.tensor.matmul(bank[:, at:at + P], ident16[:], mask_q[:], start=False, stop=True)
                last.then_inc(mx_done, 1)

            def scores(u, count, par):
                half, h, (segs, masks, _, _) = ST[u]
                pe.wait_ge(act_done, count + 1)
                for k, (j, q0, w, at) in enumerate(segs):
                    last = nc.tensor.matmul(stp[u % 2][:, at:at + w], ks[par][:, j * P:(j + 1) * P],
                                            qs[par][:, h, q0:q0 + w], start=True, stop=not masks)
                    if masks:
                        last = nc.tensor.matmul(stp[u % 2][:, masks[k]:masks[k] + P], ident16[:], mask_k[:],
                                                start=False, stop=True)
                last.then_inc(st_done, 1)

            def values(i, h, par):
                half = i // 4
                for j in range(i + 1):
                    at = prob_column(i, j)
                    nc.tensor.matmul(pvp[:, h * VW:h * VW + VW], p1[half][:, h, at:at + P], vs[par][:, j, :],
                                     start=(j == 0), stop=False)
                    last = nc.tensor.matmul(pvp[:, h * VW:h * VW + 1 + 2 * HD], p2[half][:, h, at:at + P],
                                            vs[par][:, j, 0:1 + 2 * HD], start=False, stop=(j == i))
                return last

            def fill(tu):
                pe.wait_ge(tr_free, tu + 1)

            def max_transpose(half, tu, par):
                fill(tu)
                for i in range(4):
                    last = nc.tensor.transpose(trp[0:REP, i * P:(i + 1) * P], mx[par][:, half * 4 + i, :], ident[:])
                last.then_inc(tr_full, 1)

            def burst(which, tu, src, calls):
                fill(tu)
                pe.wait_ge(w_in[which], calls)
                for kk in range(2):
                    for nb in range(2):
                        for kh in range(2):
                            r = 32 * (2 * nb + kh)
                            last = nc.tensor.matmul(trp[r:r + 32, :], src[:, kh * 4 + which * 2 + kk, :],
                                                    wch[which][:, 2 * kh + kk, nb * HALF:(nb + 1) * HALF],
                                                    start=(kk == 0), stop=(kk == 1))
                last.then_inc(tr_full, 1)

            def burst_transpose(tu):
                fill(tu)
                for cc in range(4):
                    last = nc.tensor.transpose(trp[:, cc * P:(cc + 1) * P], fsb[:, cc * P:(cc + 1) * P], ident[:])
                last.then_inc(tr_full, 1)

            def y_transpose(half, tu):
                fill(tu)
                for i in range(4):
                    last = nc.tensor.transpose(trp[:, i * P:(i + 1) * P], yn[:, half, i, :], ident[:])
                last.then_inc(tr_full, 1)

            def sums(tu, count):
                for k, v in enumerate((s1, s2)):
                    fill(tu + k)
                    pe.wait_ge(ln_sum, count + k + 1)
                    nc.tensor.matmul(trp[:, 0:B], onesd[:], v[:], start=True, stop=True).then_inc(tr_full, 1)

            pe.wait_ge(t_done, 1)
            fill(0)
            for k in range(KT):
                last = nc.tensor.transpose(trp[:, k * B:(k + 1) * B], xl[:, k * P:(k + 1) * P], ident[0:B, 0:B])
            last.then_inc(tr_full, 1)
            pe.wait_ge(qk_in[0], 32)
            for k in range(NMX):
                scores_max(k, k, 0, first=k < 2)
            pe.wait_ge(mx_free, NMX)
            max_transpose(0, 1, 0)
            burst(0, 2, t_in, 32)
            burst(1, 3, t_in, 32)
            burst_transpose(4)
            sums(5, 0)
            pe.wait_ge(init, 7)
            pe.wait_ge(init_p, 2)
            with pe.Fori(0, STEPS) as s:
                with pe.Fori(0, CH) as c:
                    for par in range(2):
                        it = s * CH + c
                        n = it * 2 + par
                        tb = trb(s, c, par)
                        for u in range(NST):
                            if u == 0:
                                pe.wait_ge(m_in[par], (it + 1) * 16)
                            if u == HALF_ST:
                                pe.wait_ge(m_in[2 + par], (it + 1) * 16)
                            scores(u, n * NST + u, par)
                            for e in PLAN[u]:
                                if e[0] == "pv":
                                    _, half, i, h = e
                                    if h == 0:
                                        pe.wait_ge(pv_free, n * NT + PV_IDX[i] + 1)
                                    if i == 4 and h == 0:
                                        pe.wait_ge(sub_done, n * NST + 4)
                                    if i == 0 and h == 0:
                                        pe.wait_ge(v_in[par], (it + 1) * 16)
                                        pe.wait_ge(sub_done, n * NST + HALF_ST + 4)
                                    last = values(i, h, par if half == 0 else 1 - par)
                                    if h == REP - 1:
                                        last.then_inc(pv_done, 1)
                                elif e[0] == "mx":
                                    if e[1] == 0:
                                        pe.wait_ge(qk_in[1 - par], (it + 1 + par) * 32)
                                    scores_max(e[1], (n + 1) * NMX + e[1], 1 - par)
                                elif e[0] == "mt":
                                    if e[1] == 1:
                                        pe.wait_ge(mx_free, (n + 1) * NMX)
                                        max_transpose(1, tb + use[e], par)
                                    else:
                                        pe.wait_ge(mx_free, (n + 1) * NMX + MX_HALF)
                                        max_transpose(0, tb + use[e], 1 - par)
                                elif e[0] == "fa":
                                    if par == 0:
                                        pe.wait_ge(t_done, s + 2)
                                    else:
                                        pe.wait_ge(h_done, it + 1)
                                    burst(0, tb + use[e], h_in if par else t_in, (n + 2) * 32)
                                elif e[0] == "fb":
                                    burst(1, tb + use[e], h_in if par else t_in, (n + 2) * 32)
                                elif e[0] == "ft":
                                    burst_transpose(tb + use[e])
                                elif e[0] == "yt":
                                    pe.wait_ge(pv_free, n * NT + (4 if e[1] == 1 else 8) + 1)
                                    y_transpose(e[1], tb + use[e])
                sums(TR0 + s * TR_STEP + NT * TRN, (s + 1) * 2)
            pe.wait_ge(sub_done, GROUPS * NST + 4)
            for i in range(4, NT):
                pe.wait_ge(pv_free, GROUPS * NT + PV_IDX[i] + 1)
                for h in range(REP):
                    last = values(i, h, 1)
                last.then_inc(pv_done, 1)
            pe.wait_ge(pv_free, GROUPS * NT + 4 + 1)
            y_transpose(1, LAST)
            pe.wait_ge(t_done, STEPS + 3)
            burst(0, LAST + 1, h_in, (GROUPS + 3) * 32)
            burst(1, LAST + 2, h_in, (GROUPS + 3) * 32)
            pe.wait_ge(t_done, STEPS + 4)
            for k in range(2 * B):
                fill(LAST + 3 + k)
                nc.tensor.matmul(trp[:], picks[:, k, :], fsb[:], start=True, stop=True).then_inc(tr_full, 1)


MT1_OUT, MT0_OUT = 5, 23
LINKS_TURN = 17
LINKS_STEP = 3


def output_phase(nc, x, woT, gate_w, gate_b, out_g, out_b, xt_d, y_d, mhalf, bcast, out):
    TILES = B * NT
    with ExitStack() as ctx:
        def sb(name, shape, dt):
            return ctx.enter_context(nc.sbuf_tensor(name, shape, dt))

        def ps(name, shape, dt):
            return ctx.enter_context(nc.psum_tensor(name, shape, dt))

        def sem(name):
            return ctx.enter_context(nc.semaphore(name))

        g1, g2 = (sb(f"g{i}", [P, KT, D], F32R) for i in (1, 2))
        o1, o2 = (sb(f"o{i}", [P, KT, D], F32R) for i in (1, 2))
        xa = [sb(f"xa{i}", [P, KT, P], F32R) for i in range(2)]
        ya = [sb(f"ya{i}", [P, KT, P], F32R) for i in range(2)]
        xs = [sb(f"xs{i}", [P, D], F32) for i in range(2)]
        a = [sb(f"a{i}", [P, D], F32) for i in range(2)]
        c = [sb(f"c{i}", [P, D], F32) for i in range(2)]
        wst = a + c
        NW = len(wst)
        vecs = sb("vecs", [P, 3, D], F32)
        bst = sb("o_bst", [P, 2, 6], F32)
        mv = sb("o_mv", [P, 2], F32)
        ve = sb("o_ve", [P, 1], F32)
        rstd = sb("o_rstd", [P, 2], F32)
        gp = [ps(f"gp{i}", [P, D], F32) for i in range(2)]
        op = [ps(f"op{i}", [P, D], F32) for i in range(2)]

        w_in = [sem(f"o_w_in{i}") for i in range(NW)]
        w1_done, w2_done, vec_in = sem("o_w1"), sem("o_w2"), sem("o_vec_in")
        xa_in, ya_in, xs_in, out_done = sem("o_xa_in"), sem("o_ya_in"), sem("o_xs_in"), [sem(f"o_out{i}") for i in range(2)]
        g_done, o_done, issue, issue_v = sem("o_g"), sem("o_o"), sem("o_issue"), sem("o_issue_v")
        link_s, ve_done, rstd_done = sem("o_link"), sem("o_ve_done"), sem("o_rstd_done")
        gb_done, gate_done, z_done, sig_done, a_done, o_free = (
            sem(f"o_{i}") for i in ("gb", "gate", "z", "sig", "a", "o_free"))
        block = ctx.enter_context(nc.Block())
        pieces = [(gate_w, g1, g2, k) for k in range(KT)] + [(woT, o1, o2, k) for k in range(KT)]

        @block.sync
        def _(sp):
            def load_x(n):
                return x[bass.ds(n * P, P), :]

            for n, (src, _, w2, k) in enumerate(pieces):
                sp.dma_start(wst[n % NW][:], src[k * P:(k + 1) * P, :]).then_inc(w_in[n % NW], 16)
                if n == 1:
                    for r, v in enumerate((gate_b, out_g, out_b)):
                        sp.dma_start(vecs[:, r, :], v.partition_broadcast(P)).then_inc(vec_in, 16)
                    sp.dma_start(xs[0][:], load_x(0)).then_inc(xs_in, 16)
                if n >= NW - 1:
                    sp.wait_ge(w2_done, n - NW + 2)
            with sp.Fori(0, TILES // 2) as m:
                for par in range(2):
                    n = m * 2 + par
                    nn = (n + 1) % TILES
                    sp.wait_ge(out_done[1 - par], m * 16 + 1 if par == 0 else m * 16 + 17)
                    sp.dma_start(xs[1 - par][:], load_x(nn)).then_inc(xs_in, 16)
                    sp.wait_ge(a_done, n + 1)
                    sp.dma_start(out[bass.ds(n * P, P), :], a[par][:]).then_inc(out_done[par], 16)
            for par in range(2):
                sp.wait_ge(out_done[par], 16 * (TILES // 2) + 1)
            sp.wait_ge(xs_in, 16 * (TILES + 1))

        @block.gpsimd
        def _(pool):
            def load_xa(nn):
                pool.sem_inc(issue, 1)
                for part in range(2):
                    nc.gpsimd.dma_start(xa[part][:], xt_d[bass.ds(nn // NT, 1), part, :, :, bass.ds((nn % NT) * P, P)]
                                        .rearrange("a p k t -> (a p) k t")).then_inc(xa_in, 16)

            def load_ya(nn):
                pool.sem_inc(issue, 1)
                for part in range(2):
                    nc.gpsimd.dma_start(ya[part][:], y_d[part, bass.ds(1 + (nn // NT) * KV, KV), :, bass.ds((nn % NT) * P, P)]
                                        .rearrange("g p t -> p g t")).then_inc(ya_in, 16)

            def power(n, k):
                pool.wait_ge(ve_done, n * 2 + k + 1)
                nc.gpsimd.tensor_tensor(rstd[:, k:k + 1], ve[:], mhalf[:, 0:1], ALU.pow).then_inc(rstd_done, 1)

            load_xa(0)
            load_ya(0)
            with pool.Fori(0, TILES) as n:
                pool.wait_ge(g_done, n + 1)
                load_xa((n + 1) % TILES)
                power(n, 0)
                power(n, 1)
                pool.wait_ge(o_done, n + 1)
                load_ya((n + 1) % TILES)
            pool.wait_ge(xa_in, 32 * (TILES + 1))
            pool.wait_ge(ya_in, 32 * (TILES + 1))

        @block.scalar
        def _(act):
            for n, (_, w1, w2, k) in enumerate(pieces):
                act.wait_ge(w_in[n % NW], 16 * (n // NW + 1))
                nc.scalar.activation(w1[:, k, :], wst[n % NW][:], ACT.Copy).then_inc(w1_done, 1)
            with act.Fori(0, TILES // 2) as m:
                for par in range(2):
                    n = m * 2 + par
                    act.wait_ge(gb_done, n + 1)
                    nc.scalar.activation(c[par][:], a[par][:], ACT.Sigmoid).then_inc(gate_done, 1)
                    act.wait_ge(z_done, n + 1)
                    nc.scalar.activation(c[par][:], a[par][:], ACT.Sigmoid).then_inc(sig_done, 1)

        @block.vector
        def _(dve):
            for w, v in ((out_done[0], 1), (out_done[1], 1), (o_free, 2)):
                dve.sem_inc(w, v)
            for n, (_, w1, w2, k) in enumerate(pieces):
                dve.wait_ge(w1_done, n + 1)
                nc.vector.tensor_tensor(w2[:, k, :], wst[n % NW][:], f32(w1[:, k, :]), ALU.subtract).then_inc(w2_done, 1)
            dve.wait_ge(w2_done, 2 * KT)
            dve.wait_ge(vec_in, 48)
            LINKS = 10
            with dve.Fori(0, TILES // 2) as m:
                for par in range(2):
                    n = m * 2 + par
                    A, C, X = a[par], c[par], xs[par]
                    count = {"n": 0}

                    def link(ins):
                        count["n"] += 1
                        ins.then_inc(link_s, 1)
                        dve.wait_ge(link_s, n * LINKS + count["n"])

                    def stats(src, eps, which):
                        for cc in range(2):
                            last = nc.vector.bn_stats(bst[:, cc, :], src[:, cc * 512:(cc + 1) * 512])
                        link(last)
                        dve.sem_inc(issue_v, 1)
                        link(nc.vector.bn_aggr(mv[:], bst[:].rearrange("p a b -> p (a b)")))
                        nc.vector.tensor_scalar(ve[:], mv[:, 1:2], eps, None, ALU.add).then_inc(ve_done, 1)
                        dve.wait_ge(rstd_done, 2 * n + which + 1)

                    dve.wait_ge(g_done, n + 1)
                    dve.wait_ge(out_done[par], m * 16 + 1)
                    nc.vector.tensor_tensor(A[:], gp[par][:], vecs[:, 0, :], ALU.add).then_inc(gb_done, 1)
                    dve.wait_ge(xs_in, 16 * (n + 1))
                    stats(X, EPS_X, 0)
                    dve.wait_ge(gate_done, n + 1)
                    link(nc.vector.tensor_scalar(A[:], X[:], mv[:, 0:1], rstd[:, 0:1], ALU.subtract, ALU.mult))
                    link(nc.vector.tensor_tensor(C[:], C[:], bcast[:, bass.ds(n // NT, 1), :]
                                                 .rearrange("p a d -> p (a d)"), ALU.mult))
                    link(nc.vector.tensor_tensor(A[:], A[:], C[:], ALU.add))
                    stats(A, EPS_F, 1)
                    link(nc.vector.tensor_scalar(A[:], A[:], mv[:, 0:1], rstd[:, 1:2], ALU.subtract, ALU.mult))
                    link(nc.vector.tensor_tensor(A[:], A[:], vecs[:, 1, :], ALU.mult))
                    nc.vector.tensor_tensor(A[:], A[:], vecs[:, 2, :], ALU.add).then_inc(z_done, 1)
                    dve.wait_ge(o_done, n + 1)
                    dve.wait_ge(z_done, n + 1)
                    dve.wait_ge(sig_done, n + 1)
                    link(nc.vector.tensor_tensor(A[:], A[:], C[:], ALU.mult))
                    nc.vector.tensor_tensor(A[:], op[par][:], A[:], ALU.mult).then_inc(o_free, 1)
                    dve.wait_ge(o_free, n + 3)
                    nc.vector.tensor_tensor(A[:], A[:], X[:], ALU.add).then_inc(a_done, 1)
                    assert count["n"] == LINKS, count

        @block.tensor
        def _(pe):
            def product(bank, lhs, ws, first):
                for k in range(KT):
                    for pa, pw in ((0, 0), (1, 0), (0, 1)):
                        if first is not None and pa == 0 and pw == 0:
                            pe.wait_ge(w2_done, first + k + 1)
                        for half in range(2):
                            cols = slice(half * HALF, (half + 1) * HALF)
                            last = nc.tensor.matmul(bank[:, cols], lhs[pa][:, k, :], ws[pw][:, k, cols],
                                                    start=(k == 0 and (pa, pw) == (0, 0)),
                                                    stop=(k == KT - 1 and (pa, pw) == (0, 1)))
                return last

            def tile(n, par, first):
                pe.wait_ge(xa_in, 32 * (n + 1))
                if not first:
                    pe.wait_ge(gb_done, n - 1)
                product(gp[par], xa, (g1, g2), 0 if first else None).then_inc(g_done, 1)
                pe.wait_ge(ya_in, 32 * (n + 1))
                pe.wait_ge(o_free, n + 1)
                product(op[par], ya, (o1, o2), KT if first else None).then_inc(o_done, 1)

            tile(0, 0, True)
            tile(1, 1, True)
            with pe.Fori(1, TILES // 2) as m:
                for par in range(2):
                    tile(m * 2 + par, par, False)


def pair_rows(w, heads):
    w = np.asarray(w).reshape(heads // 8, 8, EO, 2, D)
    return np.ascontiguousarray(w.transpose(4, 0, 3, 2, 1).reshape(D, heads * HD))


def columns(v):
    return np.ascontiguousarray(np.asarray(v).reshape(-1, P).T)


def rope_tables():
    theta = np.float32(1.0) / np.power(np.float32(10000.0), np.arange(0, HD, 2, dtype=np.float32) / np.float32(HD))
    freqs = np.arange(T, dtype=np.float32)[None, :] * theta.astype(np.float32)[:, None]
    return [np.ascontiguousarray(np.repeat(f(freqs).astype(np.float32), 8, axis=0)) for f in (np.cos, np.sin)]


def row_picks():
    pick = np.zeros((P, 2 * B, P), np.float32)
    for b in range(B):
        for nb in range(2):
            for kh in range(2):
                pick[32 * (2 * nb + kh) + b, 2 * b + nb] = 1.0
    return pick


def kernel(**inputs):
    import concourse.bacc as _bacc
    from concourse.bass_utils import run_bass_kernel_spmd as _run

    a = {k: np.asarray(v) for k, v in inputs.items()}
    f = {k.removeprefix("L0_ffn_").removeprefix("L0_attn_"): v for k, v in a.items()}
    rope_c, rope_s = rope_tables()
    row = lambda v: np.ascontiguousarray(v.reshape(1, -1))
    arrays = {
        "x": np.ascontiguousarray(f["x"].reshape(B * T, D)),
        "wqT": pair_rows(f["wq"], H), "wkT": pair_rows(f["wk"], KV),
        "wvT": np.ascontiguousarray(f["wv"].T), "woT": np.ascontiguousarray(f["wo"].T),
        "in_g": row(f["in_gamma"]), "in_b": row(f["in_beta"]),
        "agg_w": f["agg_w"], "agg_b": columns(f["agg_b"]),
        "pn_g": columns(f["pn_gamma"]), "pn_b": columns(f["pn_beta"]),
        "d1_w": f["d1_w"], "d1_b": np.ascontiguousarray(f["d1_b"].reshape(CH, KT, P).transpose(0, 2, 1)),
        "d2_w": f["d2_w"], "d2_b": columns(f["d2_b"]), "bc_w": f["bc_w"], "bc_b": row(f["bc_b"]),
        "gate_w": f["gate_w"], "gate_b": row(f["gate_b"]), "out_g": row(f["out_gamma"]), "out_b": row(f["out_beta"]),
        "rope_c": rope_c, "rope_s": rope_s, "pick": row_picks(),
    }
    nc = _bacc.Bacc("TRN2", target_bir_lowering=False, num_devices=1)
    named, aps = {}, {}
    for name, v in arrays.items():
        named[f"in_{name}"] = np.ascontiguousarray(v)
        aps[name] = nc.dram_tensor(f"in_{name}", v.shape, mybir.dt.from_np(v.dtype), kind="ExternalInput").ap()
    aps["out"] = nc.dram_tensor("out", (B * T, D), F32, kind="ExternalOutput").ap()
    build_kernel(nc, **aps)
    r = _run(nc, [named], core_ids=[0])
    return r.results[0]["out"].reshape(B, T, D)
```

```python
from contextlib import ExitStack

import numpy as np

import concourse.bass as bass
from concourse import mybir

F32 = mybir.dt.float32
F32R = mybir.dt.float32r
BF16 = mybir.dt.bfloat16
ALU = mybir.AluOpType
ACT = mybir.ActivationFunctionType
AX = mybir.AxisListType

P = 128
B, T, D = 4, 1024, 1024
H, KV, HD = 32, 8, 32
REP = H // KV
FF = 4096
STEPS = 4
KT = D // P
NT = T // P
HALF = T // 2
EO = HD // 2
PAIRS = H // 8
GROUPS = B * KV
CH = FF // D
SCALE = HD ** -0.5
NEG = -1.0e30
EPS_X, EPS_F = 1e-5, 1e-6


def f32(ap):
    return ap.bitcast(F32)


def score_units(half):
    j0, q0 = 4 * half, HALF * half
    full = [([(j, q0, HALF, 0)], [], (0, HALF), HALF * j) for j in range(j0)]
    at = HALF * j0
    return full + [
        ([(j0, q0, 512, 0)], [0], (0, 512), at),
        ([(j0 + 1, q0 + 128, 384, 0)], [0], (0, 384), at + 512),
        ([(j0 + 3, q0 + 256, 256, 0), (j0 + 2, q0 + 256, 256, 256)], [128, 256], (128, 512), at + 896),
    ]


def prob_piece(half, j):
    j0 = 4 * half
    if j < j0:
        return HALF * j, 0
    return HALF * j0 + [0, 512, 1024, 896][j - j0], P * (j - j0)


PROB_W = [1280, 3328]
ST = [(half, h, u) for half in range(2) for u in score_units(half) for h in range(REP)]
NST = len(ST)
HALF_ST = REP * 3


def max_units():
    out = []
    for i in range(NT):
        per = 4 if i < 2 else 2 if i < 4 else 1
        out += [(i, h, per) for h in range(0, REP, per)]
    return out


MX = max_units()
NMX = len(MX)
MX_HALF = sum(1 for i, _, _ in MX if i < 4)


PLAN_TEXT = """
0: mx 18
1: mx 19
2: mx 20
3: mx 21
4: pv 1 6, pv 1 7, cy 1
5: mt 1
6: pv 0 0
7: fa 0
8: fa 1, fc
9: pv 0 1
10: fb 0
11: fb 1, fs
12: pv 0 2
13: ft, mx 0
14: pv 0 3, mx 1, cy 0
15: ss 1 -1, cs 1
16: mx 2, rc 1 0
17: mx 3, rc 1 1
18: pv 1 0, rc 1 2
19: mx 4, rc 1 3
20: pv 1 1, ym 1
21: mx 5, y1 1
22: mx 6, y2 1
23: ss 0 0, ss 0 -1, cs 0
24: mx 7
25: pv 1 2, rc 0 0
26: mx 8, mt 0
27: mx 9
28: pv 1 3, rc 0 1
29: mx 10
30: mx 11, rc 0 2
31: mx 12
32: mx 13
33: pv 1 4, rc 0 3
34: mx 14
35: mx 15, ym 0
36: pv 1 5, y1 0
37: mx 16
38: mx 17, y2 0
"""


def group_plan():
    at = [[] for _ in range(NST)]
    for row in PLAN_TEXT.split("\n"):
        if row:
            slot, entries = row.split(": ")
            for entry in entries.split(", "):
                what, *numbers = entry.split(" ")
                at[int(slot)].append((what, *(int(v) for v in numbers)))
    return at


PLAN = group_plan()
PV_ORDER = [e[1:] for slot in PLAN for e in slot if e[0] == "pv"]
NPV = len(PV_ORDER)
CARRIED = [(1, 6), (1, 7)]
MX_LATE = 18
SUMS = [[0, -1], [-1]]
LAST_UNIT = {(0, 0): 3, (0, 1): 7, (0, 2): 11, (0, 3): 11, (1, 0): 15, (1, 1): 19, (1, 2): 23, (1, 3): 27,
             (1, 4): 31, (1, 5): 35}
NADD = 7
TRN = 7


def build_kernel(nc, x, wqT, wkT, wvT, woT, in_g, in_b, agg_w, agg_b, pn_g, pn_b, d1_w, d1_b, d2_w, d2_b,
                 bc_b, gate_w, gate_b, out_g, out_b, rope_c, rope_s, pick, out):
    def dram(name, shape, dt):
        return nc.dram_tensor(name, shape, dt, kind="Internal").ap()

    xt_d = dram("xt_scratch", (B, 2, P, KT, T), F32)
    q_d = dram("q_scratch", (B * PAIRS, 2, 2, P, T), F32)
    k_d = dram("k_scratch", (B, 2, 2, P, T), F32)
    v_d = dram("v_scratch", (GROUPS, P, NT, HD), F32)
    y_d = dram("y_scratch", (2, 1 + GROUPS, P, T), F32)

    with ExitStack() as outer:
        def osb(name, shape, dt):
            return outer.enter_context(nc.sbuf_tensor(name, shape, dt))

        ident = osb("ident", [P, P], F32)
        ident16 = osb("ident16", [P, P], BF16)
        mask_q = osb("mask_q", [P, P], BF16)
        mask_k = osb("mask_k", [P, P], BF16)
        mhalf = osb("mhalf", [P, 4], F32)

        project_phase(nc, x, wqT, wkT, wvT, rope_c, rope_s, xt_d, q_d, k_d, v_d,
                      ident, ident16, mask_q, mask_k, mhalf)
        bcast = osb("bcast", [P, B, D], F32)
        attention_phase(nc, x, in_g, in_b, agg_w, agg_b, pn_g, pn_b, d1_w, d1_b, d2_w, d2_b, bc_b, pick,
                        q_d, k_d, v_d, y_d, ident, ident16, mask_q, mask_k, mhalf, bcast)
        output_phase(nc, x, woT, gate_w, gate_b, out_g, out_b, xt_d, y_d, mhalf, bcast, out)


def project_phase(nc, x, wqT, wkT, wvT, rope_c, rope_s, xt_d, q_d, k_d, v_d,
                  ident, ident16, mask_q, mask_k, mhalf):
    NB = 2 * B
    NP = PAIRS + 1
    QK = PAIRS * 256
    WN = QK + 256 + KV * HD
    with ExitStack() as ctx:
        def sb(name, shape, dt):
            return ctx.enter_context(nc.sbuf_tensor(name, shape, dt))

        def ps(name, shape, dt):
            return ctx.enter_context(nc.psum_tensor(name, shape, dt))

        def sem(name):
            return ctx.enter_context(nc.semaphore(name))

        w1 = sb("w1", [P, KT, WN], F32R)
        w2 = sb("w2", [P, KT, WN], F32R)
        xin = sb("xin", [P, 4, D], F32)
        xt = [[sb(f"xt{p}{i}", [P, KT, HALF], F32R) for i in range(2)] for p in range(2)]
        cs = sb("cs", [P, 2, T], F32)
        rt = sb("rt", [P, 4, HALF], F32)
        r1 = sb("r1", [P, 2, HALF], F32R)
        r2 = sb("r2", [P, 2, HALF], F32R)
        vo = sb("vo", [P, KV, 4, HD], F32)
        bst = sb("bst", [P, 4, 2, 6], F32)
        mv = sb("mv", [P, 4, 2], F32)
        ve = sb("ve", [P, 4], F32)
        rstd = sb("rstd", [P, 4], F32)
        tr = [ps(f"tr{i}", [P, HALF], F32) for i in range(2)]
        eo = [ps(f"eo{i}", [P, 2, HALF], F32) for i in range(2)]
        pv = [ps(f"pv{i}", [P, 512], F32) for i in range(2)]

        const_ready = sem("p_const")
        w_in, w1_done, w2_done = [sem(f"p_w_in{i}") for i in range(4)], sem("p_w1"), sem("p_w2")
        cs_in = sem("p_cs_in")
        x_in, stats_done, rstd_done, xn_done = sem("p_x_in"), sem("p_stats"), sem("p_rstd"), sem("p_xn")
        stat_link, issue = sem("p_link"), sem("p_issue")
        tr_done, x1_done, x2_done = sem("p_tr"), sem("p_x1"), sem("p_x2")
        xt_out = [sem(f"p_xt_out{i}") for i in range(2)]
        pair_done, mul_done, rope_done = sem("p_pair"), sem("p_mul"), sem("p_rope")
        r1_done, r2_done, r_out = sem("p_r1"), sem("p_r2"), sem("p_r_out")
        v_done, vo_done, v_out = sem("p_v"), sem("p_vo"), sem("p_v_out")
        block = ctx.enter_context(nc.Block())

        rtf, csf = (v[:].rearrange("p a t -> p (a t)") for v in (rt, cs))
        r1f, r2f = (f32(v[:]).rearrange("p a t -> p (a t)") for v in (r1, r2))
        vof = vo[:].rearrange("p g t d -> p (g t d)")
        wst = [(rtf[:, 0:QK], rtf[:, QK:WN]), (csf[:, 0:QK], csf[:, QK:WN]),
               (r1f, vof[:, 0:WN - QK]), (r2f, vof[:, WN - QK:2 * (WN - QK)])]
        NW = len(wst)
        parts = ((0, QK), (QK, WN))
        srcs = [(wqT, 0, 0, QK), (wkT, 1, 0, 256), (wvT, 1, 256, KV * HD)]

        def x_block(n):
            return x[bass.ds(n * HALF, HALF)].rearrange("(t p) d -> p t d", p=P)

        @block.sync
        def _(sp):
            sp.dma_start(xin[:], x_block(0)).then_inc(x_in, 16)
            for k in range(KT):
                if k >= NW:
                    sp.wait_ge(w2_done, k - NW + 1)
                for src, place, c0, w in srcs:
                    sp.dma_start(wst[k % NW][place][:, c0:c0 + w], src[k * P:(k + 1) * P, :]).then_inc(w_in[k % NW], 16)
            sp.wait_ge(w2_done, KT)
            sp.dma_start(cs[:, 0, :], rope_c).then_inc(cs_in, 16)
            sp.dma_start(cs[:, 1, :], rope_s).then_inc(cs_in, 16)
            sp.wait_ge(tr_done, KT)
            sp.dma_start(xin[:], x_block(1)).then_inc(x_in, 16)
            def turn(b, final):
                for half in range(2):
                    n = 2 * b + half
                    sp.wait_ge(x2_done, KT * n + KT)
                    for p in range(2):
                        sp.dma_start(xt_d[bass.ds(b, 1), p, :, :, half * HALF:(half + 1) * HALF]
                                     .rearrange("a p k t -> (a p) k t"), f32(xt[p][half][:])).then_inc(xt_out[half], 16)
                    for q in range(NP):
                        sp.wait_ge(r2_done, NP * n + q + 2)
                        dst, blk = (q_d, b * PAIRS + q) if q < PAIRS else (k_d, b)
                        for part, r in enumerate((r1, r2)):
                            sp.dma_start(dst[bass.ds(blk, 1), part, :, :, half * HALF:(half + 1) * HALF]
                                         .rearrange("a e p t -> (a p) e t"), f32(r[:])).then_inc(r_out, 16)
                    if not final:
                        sp.wait_ge(tr_done, KT * n + 2 * KT)
                        sp.dma_start(xin[:], x_block(n + 2)).then_inc(x_in, 16)
                    sp.wait_ge(vo_done, 4 * n + 4 + 2)
                    sp.dma_start(v_d[bass.ds(b * KV, KV), :, half * 4:half * 4 + 4, :].rearrange("g p t d -> p g (t d)"),
                                 vo[:].rearrange("p g t d -> p g (t d)")).then_inc(v_out, 16)

            with sp.Fori(0, B - 1) as b:
                turn(b, False)
            turn(B - 1, True)
            sp.wait_ge(x_in, 16 * NB)
            for i in range(2):
                sp.wait_ge(xt_out[i], 32 * B + 1)
            sp.wait_ge(v_out, 16 * NB + 1)
            sp.wait_ge(r_out, 32 * NP * NB + 1)

        @block.gpsimd
        def _(pool):
            nc.gpsimd.memset(mhalf[:], -0.5).then_inc(const_ready, 1)
            nc.gpsimd.memset(ident[:], 0.0).then_inc(const_ready, 1)
            nc.gpsimd.memset(mask_q[:], 0.0).then_inc(const_ready, 1)
            nc.gpsimd.memset(mask_k[:], 0.0).then_inc(const_ready, 1)
            pool.wait_ge(const_ready, 4)
            nc.gpsimd.affine_select(out=ident[:], in_=ident[:], compare_op=ALU.not_equal, fill=1.0, base=0,
                                    pattern=[[-1, P]], channel_multiplier=1).then_inc(const_ready, 1)
            nc.gpsimd.affine_select(out=mask_q[:], in_=mask_q[:], compare_op=ALU.is_ge, fill=NEG, base=0,
                                    pattern=[[-1, P]], channel_multiplier=1).then_inc(const_ready, 1)
            nc.gpsimd.affine_select(out=mask_k[:], in_=mask_k[:], compare_op=ALU.is_ge, fill=NEG, base=0,
                                    pattern=[[1, P]], channel_multiplier=-1).then_inc(const_ready, 1)
            pool.wait_ge(const_ready, 7)
            nc.gpsimd.tensor_copy(ident16[:], ident[:]).then_inc(const_ready, 1)

            def rstd_of(n):
                pool.wait_ge(stats_done, n + 1)
                nc.gpsimd.tensor_tensor(rstd[:], ve[:], mhalf[:], ALU.pow).then_inc(rstd_done, 1)

            rstd_of(0)

            def turn(b, final):
                for half in range(2):
                    n = 2 * b + half
                    if not (final and half):
                        rstd_of(n + 1)
                    for q in range(NP):
                        pool.wait_ge(r1_done, NP * n + q + 1)
                        nc.gpsimd.tensor_tensor(r2[:], rt[:, 0:2, :], f32(r1[:]), ALU.subtract).then_inc(r2_done, 1)

            with pool.Fori(0, B - 1) as b:
                turn(b, False)
            turn(B - 1, True)

        @block.scalar
        def _(act):
            def round_x(m, par, k):
                act.wait_ge(tr_done, KT * m + k + 1)
                nc.scalar.activation(xt[0][par][:, k, :], tr[k % 2][:], ACT.Copy).then_inc(x1_done, 1)

            for k in range(KT):
                act.wait_ge(w_in[k % NW], 48 * (k // NW + 1))
                for place, (c0, c1) in enumerate(parts):
                    last = nc.scalar.activation(w1[:, k, c0:c1], wst[k % NW][place], ACT.Copy)
                last.then_inc(w1_done, 1)
                round_x(0, 0, k)
            def turn(b, final):
                for half in range(2):
                    n = 2 * b + half
                    for q in range(NP):
                        for k in x_tiles(q, final and half):
                            if k == 0 and half == 0:
                                act.wait_ge(xt_out[1], 32 * b + 1)
                            elif k == 0:
                                act.wait_ge(xt_out[0], 32 * b + 33)
                            round_x(n + 1, 1 - half, k)
                        act.wait_ge(rope_done, NP * n + q + 1)
                        act.wait_ge(r_out, 32 * (NP * n + q) + 1)
                        nc.scalar.activation(r1[:], rt[:, 0:2, :], ACT.Copy).then_inc(r1_done, 1)
                    for t in range(4):
                        act.wait_ge(v_done, 4 * n + t + 1)
                        if t == 0:
                            act.wait_ge(v_out, 16 * n + 1)
                        nc.scalar.activation(vo[:, :, t, :], pv[t % 2][:, 0:KV * HD]
                                             .rearrange("p (g d) -> p g d", g=KV), ACT.Copy).then_inc(vo_done, 1)
                        for k in x_tiles(NP + t, final and half):
                            round_x(n + 1, 1 - half, k)

            with act.Fori(0, B - 1) as b:
                turn(b, False)
            turn(B - 1, True)

        @block.vector
        def _(dve):
            for w, v in ((r_out, 1), (xt_out[0], 1), (xt_out[1], 1), (v_out, 1), (r2_done, 1),
                         (mul_done, 2), (vo_done, 2)):
                dve.sem_inc(w, v)

            def statistics(m):
                dve.wait_ge(x_in, 16 * (m + 1))
                for t in range(4):
                    for c in range(2):
                        last = nc.vector.bn_stats(bst[:, t, c, :], xin[:, t, c * 512:(c + 1) * 512])
                last.then_inc(stat_link, 1)
                dve.wait_ge(stat_link, 2 * m + 1)
                dve.sem_inc(issue, 1)
                for t in range(4):
                    last = nc.vector.bn_aggr(mv[:, t, :], bst[:, t].rearrange("p a b -> p (a b)"))
                last.then_inc(stat_link, 1)
                dve.wait_ge(stat_link, 2 * m + 2)
                nc.vector.tensor_scalar(ve[:], mv[:, :, 1], EPS_X, None, ALU.add).then_inc(stats_done, 1)

            def normalise(m):
                dve.wait_ge(rstd_done, m + 1)
                for t in range(4):
                    nc.vector.tensor_scalar(xin[:, t, :], xin[:, t, :], mv[:, t, 0:1], rstd[:, t:t + 1],
                                            ALU.subtract, ALU.mult).then_inc(xn_done, 1)

            def rest_x(m, par, k):
                dve.wait_ge(x1_done, KT * m + k + 1)
                nc.vector.tensor_tensor(xt[1][par][:, k, :], tr[k % 2][:], f32(xt[0][par][:, k, :]),
                                        ALU.subtract).then_inc(x2_done, 1)

            statistics(0)
            normalise(0)
            for k in range(KT):
                dve.wait_ge(w1_done, k + 1)
                for place, (c0, c1) in enumerate(parts):
                    last = nc.vector.tensor_tensor(w2[:, k, c0:c1], wst[k % NW][place], f32(w1[:, k, c0:c1]), ALU.subtract)
                last.then_inc(w2_done, 1)
                rest_x(0, 0, k)
            dve.wait_ge(cs_in, 32)

            def turn(b, final):
                for half in range(2):
                    n = 2 * b + half
                    tok = slice(half * HALF, (half + 1) * HALF)
                    for q in range(NP):
                        if q == 1 and not (final and half):
                            normalise(n + 1)
                        for k in x_tiles(q, final and half):
                            rest_x(n + 1, 1 - half, k)
                        bank = eo[(half + q) % 2]
                        dve.wait_ge(pair_done, NP * n + q + 1)
                        dve.wait_ge(r2_done, NP * n + q + 1)
                        for o, e, s in ((0, 0, 0), (1, 0, 1), (2, 1, 1), (3, 1, 0)):
                            last = nc.vector.tensor_tensor(rt[:, o, :], bank[:, e, :], cs[:, s, tok], ALU.mult)
                        last.then_inc(mul_done, 1)
                        dve.wait_ge(mul_done, NP * n + q + 3)
                        nc.vector.tensor_tensor(rt[:, 0, :], rt[:, 0, :], rt[:, 2, :], ALU.subtract)
                        nc.vector.tensor_tensor(rt[:, 1, :], rt[:, 1, :], rt[:, 3, :], ALU.add).then_inc(rope_done, 1)
                        if q == 0 and not (final and half):
                            statistics(n + 1)
                    for t in range(4):
                        for k in x_tiles(NP + t, final and half):
                            rest_x(n + 1, 1 - half, k)

            with dve.Fori(0, B - 1) as b:
                turn(b, False)
            turn(B - 1, True)

        @block.tensor
        def _(pe):
            def transpose_x(m, k, first=False):
                if k == 0:
                    pe.wait_ge(xn_done, 4 * m + 4)
                if not (first and k < 2):
                    pe.wait_ge(x2_done, KT * m + k - 1)
                for t in range(4):
                    last = nc.tensor.transpose(tr[k % 2][:, t * P:(t + 1) * P], xin[:, t, k * P:(k + 1) * P], ident[:])
                last.then_inc(tr_done, 1)

            def product(out, lhs, rhs):
                parts = [(0, 0), (0, 1), (1, 0)]
                for k in range(KT):
                    for a, c in parts:
                        last = nc.tensor.matmul(out, lhs[a](k), rhs[c](k), start=(k == 0 and (a, c) == (0, 0)),
                                                stop=(k == KT - 1 and (a, c) == (1, 0)))
                return last

            ws = (w1, w2)
            pe.wait_ge(const_ready, 8)
            for k in range(KT):
                transpose_x(0, k, first=True)
            pe.wait_ge(w2_done, KT)
            def turn(b, final):
                for half in range(2):
                    n = 2 * b + half
                    xs = [lambda k, p=p: xt[p][half][:, k, :] for p in range(2)]
                    pe.wait_ge(x2_done, KT * n + KT)
                    for q in range(NP):
                        bank = eo[(half + q) % 2]
                        pe.wait_ge(mul_done, NP * n + q + 1)
                        for e in range(2):
                            c0 = q * 256 + e * P
                            last = product(bank[:, e, :], [lambda k, w=w: w[:, k, c0:c0 + P] for w in ws], xs)
                            if e == 1:
                                last.then_inc(pair_done, 1)
                            for k in x_tiles(q, final and half)[e:e + 1]:
                                transpose_x(n + 1, k)
                    for t in range(4):
                        pe.wait_ge(vo_done, 4 * n + t + 1)
                        last = product(pv[t % 2][:, 0:KV * HD],
                                       [lambda k, p=p: xt[p][half][:, k, t * P:(t + 1) * P] for p in range(2)],
                                       [lambda k, w=w: w[:, k, QK + 256:WN] for w in ws])
                        last.then_inc(v_done, 1)
                        for k in x_tiles(NP + t, final and half):
                            transpose_x(n + 1, k)

            with pe.Fori(0, B - 1) as b:
                turn(b, False)
            turn(B - 1, True)


X_TR = [[], [], [0, 1], [2, 3], [4, 5], [6], [7], [], []]


def x_tiles(step, last_block):
    return [] if last_block else X_TR[step]


def attention_phase(nc, x, in_g, in_b, agg_w, agg_b, pn_g, pn_b, d1_w, d1_b, d2_w, d2_b, bc_b, pick,
                    q_d, k_d, v_d, y_d, ident, ident16, mask_q, mask_k, mhalf, bcast):
    QR = 3 * HD
    with ExitStack() as ctx:
        def sb(name, shape, dt):
            return ctx.enter_context(nc.sbuf_tensor(name, shape, dt))

        def ps(name, shape, dt):
            return ctx.enter_context(nc.psum_tensor(name, shape, dt))

        def sem(name):
            return ctx.enter_context(nc.semaphore(name))

        qs = [sb(f"qs{i}", [QR + 1, REP, T], F32R) for i in range(2)]
        ks = [sb(f"ks{i}", [QR + 1, T], F32R) for i in range(2)]
        vs = [sb(f"vs{i}", [P, NT, HD], F32) for i in range(2)]
        pr = [sb(f"pr{i}", [P, REP, PROB_W[i]], F32) for i in range(2)]
        acc = sb("acc", [P, REP, HALF], F32)
        acc0 = sb("acc0", [P, REP, HALF - P], F32)
        ones = sb("ones", [P, HD], F32)
        mx = [sb(f"mx{i}", [P, NT, REP], F32) for i in range(2)]
        mt = [sb(f"mt{i}", [REP, HALF], F32R) for i in range(2)]
        rinv = sb("rinv", [P, HALF], F32)
        sm = sb("sm", [P, HALF], F32)
        ys = [sb(f"ys{i}", [P, HALF], F32) for i in range(2)]
        yf = sb("yf", [P, HALF], F32)
        y1 = [sb(f"y1_{i}", [P, HALF], F32R) for i in range(2)]
        y2 = [sb(f"y2_{i}", [P, HALF], F32R) for i in range(2)]
        wch = [sb(f"wch{i}", [P, 4, D], F32) for i in range(2)]
        fsb = sb("fsb", [P, HALF], F32)
        fr = sb("fr", [P, KT, B], F32)
        hpre = sb("hpre", [P, KT, B], F32)
        b1c = sb("b1c", [P, KT], F32)
        t_in = sb("t_in", [P, KT, 32], F32)
        h_in = sb("h_in", [P, KT, 32], F32)
        th = sb("th", [P, KT, B], F32)
        cen = sb("cen", [P, KT, B], F32)
        sq = sb("sq", [P, KT, B], F32)
        s1 = sb("s1", [P, B], F32)
        s2 = sb("s2", [P, B], F32)
        ve = sb("f_ve", [P, B], F32)
        rs = sb("f_rs", [P, B], F32)
        onesd = sb("onesd", [P, P], F32)
        fvec = sb("fvec", [P, 4, KT], F32)
        fbias = sb("fbias", [P, HALF], F32)
        picks = pr[0][:, 0, 0:2 * B * P]
        lst = sb("lst", [B, 2, 6], F32)
        lmv = sb("lmv", [B, 2], F32)
        lve = sb("lve", [B, 1], F32)
        lrs = sb("lrs", [B, 1], F32)
        xl, gl, bl = (pr[0][0:B, r, 0:D] for r in range(3))

        mxp = [ps(f"mxp{i}", [P, 2 * HALF], F32) for i in range(2)]
        stp = [ps(f"stp{i}", [P, HALF], F32) for i in range(2)]
        yp = ps("yp", [P, HALF], F32)
        trp = ps("trp", [P, 512], F32)

        qk_in = [sem(f"a_qk_in{i}") for i in range(2)]
        v_in = [sem(f"a_v_in{i}") for i in range(2)]
        m_in = [sem(f"a_m_in{i}") for i in range(4)]
        w_in = [sem(f"a_w_in{i}") for i in range(2)]
        y_out = [sem(f"a_y_out{i}") for i in range(2)]
        b1_in, c_in = sem("a_b1_in"), sem("a_c_in")
        xl_in, gb_in = sem("a_xl_in"), sem("a_gb_in")
        issue = sem("a_issue")
        init, init_p = sem("a_init"), sem("a_init_p")
        pick_done, bcast_done = sem("a_pick"), sem("a_bcast")
        st_done, act_done, add_done, add0_done = sem("a_st"), sem("a_act"), sem("a_add"), sem("a_add0")
        mx_done, mx_free = sem("a_mx"), sem("a_mx_free")
        pv_done, ys_done, rc_done, yf_done, y2_done = (sem(f"a_{i}") for i in ("pv", "ys", "rc", "yf", "y2"))
        tr_full, tr_free, y1_done = sem("a_tr_full"), sem("a_tr_free"), sem("a_y1")
        hp_done, h_done, t_done = sem("a_hp"), sem("a_h"), sem("a_t")
        ln_sum, ln_ve, ln_rs = sem("a_ln_sum"), sem("a_ln_ve"), sem("a_ln_rs")
        link_s = sem("a_link")
        l_ve, l_rs = sem("a_l_ve"), sem("a_l_rs")
        block = ctx.enter_context(nc.Block())

        TR0 = 7
        TR_STEP = NT * TRN + 2

        def trb(s, c, par):
            return TR0 + s * TR_STEP + (2 * c + par) * TRN

        use = {("mt", 1): 0, "fa": 1, "fb": 2, "ft": 3, ("ss", 1): 4, ("ss", 0): 5, ("mt", 0): 6}

        def products(e, n):
            return NPV * n + PV_ORDER.index(e) + 2
        LAST = TR0 + STEPS * TR_STEP

        @block.sync
        def _(sp):
            def load_v(par, m):
                sp.dma_start(vs[par][:], v_d[bass.ds(m, 1)].rearrange("a p t d -> (a p) t d")).then_inc(v_in[par], 16)

            def load_w(burst, src):
                for kh in range(2):
                    sp.dma_start(wch[burst][:, 2 * kh:2 * kh + 2, :], src(kh * 512 + burst * 256)
                                 .rearrange("(k p) n -> p k n", p=P)).then_inc(w_in[burst], 16)

            def whole(w):
                return lambda r: w[r:r + 256, :]

            def d1_chunk(c):
                return lambda r: d1_w[r:r + 256, bass.ds(c * D, D)]

            def d2_chunk(c):
                return lambda r: d2_w[bass.ds(c * D + r, 256), :]

            def store_y(half, slot):
                for part, y in enumerate((y1, y2)):
                    sp.dma_start(y_d[part, bass.ds(slot, 1), :, half * HALF:(half + 1) * HALF]
                                 .rearrange("a p t -> (a p) t"), f32(y[half][:])).then_inc(y_out[half], 16)

            xlast = x.rearrange("(b t) d -> b t d", b=B)[:, T - 1, :]
            sp.dma_start(xl, xlast).then_inc(xl_in, 16)
            for r in range(B):
                sp.dma_start(gl[r:r + 1, :], in_g).then_inc(gb_in, 16)
                sp.dma_start(bl[r:r + 1, :], in_b).then_inc(gb_in, 16)
            load_v(0, 0)
            for r, v in enumerate((agg_b, pn_g, pn_b, d2_b)):
                sp.dma_start(fvec[:, r, :], v).then_inc(c_in, 16)
            sp.dma_start(b1c[:], d1_b[0]).then_inc(b1_in, 16)
            load_w(0, whole(agg_w))
            load_w(1, whole(agg_w))
            sp.wait_ge(init, 1)
            for nb in range(2):
                for r in range(B):
                    sp.dma_start(fbias[64 * nb + r:64 * nb + r + 1, :], bc_b[:, nb * HALF:(nb + 1) * HALF]).then_inc(c_in, 16)
            sp.wait_ge(tr_full, 3)
            load_w(0, d1_chunk(0))
            sp.wait_ge(tr_full, 4)
            load_w(1, d1_chunk(0))
            with sp.Fori(0, STEPS) as s:
                with sp.Fori(0, CH) as c:
                    for par in range(2):
                        it = s * CH + c
                        n = it * 2 + par
                        nxt = 1 - par
                        tb = trb(s, c, par)
                        sp.wait_ge(pv_done, products((1, 7), n))
                        load_v(nxt, (n + 1) % GROUPS)
                        sp.wait_ge(tr_full, tb + use["fa"] + 1)
                        cn = (c + par) % CH
                        cw = (cn + CH * ((it + 1) // (STEPS * CH))) % (CH + 1)
                        load_w(0, d2_chunk(c) if par == 0 else d1_chunk(cw))
                        sp.wait_ge(tr_full, tb + use["fb"] + 1)
                        load_w(1, d2_chunk(c) if par == 0 else d1_chunk(cw))
                        if par == 1:
                            sp.wait_ge(hp_done, it + 1)
                            sp.dma_start(b1c[:], d1_b[bass.ds(cn, 1)].rearrange("a p k -> (a p) k")).then_inc(b1_in, 16)
                        sp.wait_ge(y2_done, 2 * n + 2)
                        store_y(1, n)
                        sp.wait_ge(y2_done, 2 * n + 3)
                        store_y(0, n + 1)
            sp.wait_ge(tr_full, LAST)
            sp.dma_start(picks, pick).then_inc(c_in, 16)
            sp.wait_ge(y2_done, 2 * GROUPS + 2)
            store_y(1, GROUPS)
            for half in range(2):
                sp.wait_ge(y_out[half], 32 * (GROUPS + 1 - (1 - half)) + 1)
            for par in range(2):
                sp.wait_ge(v_in[par], 16 * (GROUPS // 2 + (1 - par)))
                sp.wait_ge(w_in[par], 32 * (GROUPS + 2))
            sp.wait_ge(b1_in, 16 * (GROUPS // 2 + 1))

        @block.gpsimd
        def _(pool):
            def load_qk(par, blk, m):
                pool.sem_inc(issue, 1)
                heads = slice(par * REP * T, (par + 1) * REP * T)
                for p0, part in ((0, 0), (HD, 0), (2 * HD, 1)):
                    nc.gpsimd.dma_start(qs[par][p0:p0 + HD].rearrange("p h t -> p (h t)"),
                                        q_d[bass.ds(blk, 1), part].rearrange("a e (f g) t -> (a e f) (g t)", g=2 * REP)
                                        [:, heads]).then_inc(qk_in[par], 16)
                for p0, np_, part in ((0, 2 * HD, slice(0, 2)), (2 * HD, HD, slice(0, 1))):
                    nc.gpsimd.dma_start(ks[par][p0:p0 + np_], k_d[bass.ds(m // KV, 1), part]
                                        .rearrange("a r e (f g) t -> (a r e f) g t", g=KV)[:, bass.ds(m % KV, 1), :]
                                        .rearrange("p g t -> p (g t)")).then_inc(qk_in[par], 16)

            def move_mt(half, par):
                pool.sem_inc(issue, 1)
                nc.gpsimd.dma_start(qs[par][QR:QR + 1, :, half * HALF:(half + 1) * HALF],
                                    f32(mt[half][:])).then_inc(m_in[2 * half + par], 16)

            load_qk(0, 0, 0)
            nc.gpsimd.memset(fbias[:], 0.0).then_inc(init, 1)
            for t in (t_in, h_in):
                nc.gpsimd.memset(t[:], 0.0).then_inc(init, 1)
            nc.gpsimd.memset(onesd[:], 1.0 / D).then_inc(init, 1)
            for k in range(2):
                pool.wait_ge(l_ve, k + 1)
                nc.gpsimd.tensor_tensor(lrs[:], lve[:], mhalf[0:B, 0:1], ALU.pow).then_inc(l_rs, 1)
            for i in range(2):
                pool.wait_ge(init, 4 + i)
                nc.gpsimd.memset(f32(ks[i][QR:QR + 1, :]), 1.0).then_inc(init, 1)
            pool.wait_ge(init, 6)
            nc.gpsimd.memset(vs[1][:], 1.0).then_inc(init, 1)
            nc.gpsimd.memset(ones[:], 1.0).then_inc(init, 1)
            nc.gpsimd.memset(acc[:], 1.0).then_inc(init_p, 1)

            def ln_pool(k):
                pool.wait_ge(ln_ve, k + 1)
                nc.gpsimd.tensor_tensor(rs[:], ve[:], mhalf[:], ALU.pow).then_inc(ln_rs, 1)

            def late_additions(n):
                pool.wait_ge(act_done, NST * n + 2)
                for k, j in enumerate((5, 6, 7)):
                    at, c0 = prob_piece(1, j)
                    pool.wait_ge(add_done, NADD * n + k + 1)
                    nc.gpsimd.tensor_tensor(acc[:, :, c0:HALF], acc[:, :, c0:HALF], pr[1][:, :, at:at + HALF - c0],
                                            ALU.add).then_inc(add_done, 1)

            pool.wait_ge(tr_free, 3)
            move_mt(0, 0)
            ln_pool(0)
            with pool.Fori(0, STEPS) as s:
                with pool.Fori(0, CH) as c:
                    for par in range(2):
                        it = s * CH + c
                        n = it * 2 + par
                        tb = trb(s, c, par)
                        for u in range(NST):
                            if u == MT1_OUT:
                                pool.wait_ge(tr_free, tb + use[("mt", 1)] + 2)
                                move_mt(1, par)
                            if u == MT0_OUT:
                                pool.wait_ge(tr_free, tb + use[("mt", 0)] + 2)
                                move_mt(0, 1 - par)
                            if u == 1:
                                pool.wait_ge(st_done, NST * n + 2)
                                load_qk(1 - par, it if par == 0 else (it + 1) % (GROUPS // 2), (n + 1) % GROUPS)
                            if u == ADD_LATE:
                                late_additions(n)
                            if u == ADD_FIRST:
                                pool.wait_ge(tr_full, tb)
                                for j in (1, 2, 3):
                                    at, c0 = prob_piece(0, j)
                                    if j > 1:
                                        pool.wait_ge(add0_done, 3 * n + j - 1)
                                    pool.wait_ge(act_done, NST * n + LAST_UNIT[(0, j)] + 3)
                                    other = pr[0][:, :, P:HALF] if j == 1 else acc0[:, :, c0 - P:HALF - P]
                                    nc.gpsimd.tensor_tensor(acc0[:, :, c0 - P:HALF - P], other, pr[0][:, :, at:at + HALF - c0],
                                                            ALU.add).then_inc(add0_done, 1)
                            if u in ADD_AT:
                                j = ADD_AT[u]
                                at = prob_piece(1, j)[0]
                                if j == 1:
                                    pool.wait_ge(tr_full, tb + use[("ss", 1)] + 1)
                                else:
                                    pool.wait_ge(add_done, NADD * n + 3 + j)
                                pool.wait_ge(act_done, NST * n + u + 3)
                                other = pr[1][:, :, 0:HALF] if j == 1 else acc[:]
                                nc.gpsimd.tensor_tensor(acc[:], other, pr[1][:, :, at:at + HALF], ALU.add).then_inc(add_done, 1)
                ln_pool(s + 1)
            late_additions(GROUPS)
            for par in range(2):
                pool.wait_ge(qk_in[par], 80 * (GROUPS // 2 + (1 - par)))
            pool.wait_ge(m_in[0], 16 * (GROUPS // 2 + 1))

        @block.scalar
        def _(act):
            def copy_burst(tu):
                act.wait_ge(tr_full, tu + 1)
                nc.scalar.activation(fsb[:], trp[:], ACT.Copy).then_inc(tr_free, 1)

            def max_rows(half, tu):
                act.wait_ge(tr_full, tu + 1)
                nc.scalar.activation(mt[half][:], trp[0:REP, :], ACT.Copy).then_inc(tr_free, 1)

            def copy_y(half, k, pieces):
                act.wait_ge(pv_done, pieces)
                act.wait_ge(yf_done, k + half)
                nc.scalar.activation(ys[half][:], yp[:], ACT.Copy).then_inc(ys_done, 1)

            def copy_sums(k, tu):
                act.wait_ge(tr_full, tu + 1)
                act.wait_ge(yf_done, k + 1)
                nc.scalar.activation(sm[:], trp[:], ACT.Copy).then_inc(tr_free, 1)

            def round_y(half, k, n):
                act.wait_ge(yf_done, k + 2)
                act.wait_ge(y_out[half], n * 32 + 1)
                nc.scalar.activation(y1[half][:], yf[:], ACT.Copy).then_inc(y1_done, 1)

            max_rows(0, 1)
            copy_burst(2)
            with act.Fori(0, STEPS) as s:
                with act.Fori(0, CH) as c:
                    for par in range(2):
                        it = s * CH + c
                        n = it * 2 + par
                        tb = trb(s, c, par)
                        for u, (half, h, (_, _, (c0, c1), at)) in enumerate(ST):
                            w = c1 - c0
                            act.wait_ge(st_done, NST * n + u + 2)
                            if u == 0:
                                act.wait_ge(tr_full, tb)
                            if u == HALF_ST:
                                act.wait_ge(pv_done, NPV * n + 1)
                                act.wait_ge(add_done, NADD * n + 1)
                            if u == NST - 2 * REP:
                                act.wait_ge(tr_full, tb + use[("ss", 1)] + 1)
                            nc.scalar.activation(pr[half][:, h, at:at + w], stp[u % 2][:, c0:c1], ACT.Exp,
                                                 scale=SCALE).then_inc(act_done, 1)
                            for e in (PLAN[u - 1] if u else []):
                                k = 2 * n + 1 - e[1] if len(e) > 1 else None
                                if e[0] == "fc":
                                    copy_burst(tb + use["fa"])
                                elif e[0] == "cy":
                                    copy_y(e[1], k, products((1, 7) if e[1] else (0, 3), n))
                                elif e[0] == "cs":
                                    copy_sums(k, tb + use[("ss", e[1])])
                                elif e[0] == "y1":
                                    round_y(e[1], k, n)
                                elif e[0] == "mt":
                                    if e[1] == 0:
                                        act.wait_ge(m_in[par], (it + 1) * 16)
                                    elif par == 1:
                                        act.wait_ge(m_in[2], (it + 1) * 16)
                                    else:
                                        act.wait_ge(st_done, n * NST + 1)
                                    max_rows(e[1], tb + use[e])
                                elif e[0] == "ft" and par == 0:
                                    act.wait_ge(hp_done, it + 1)
                                    nc.scalar.activation(h_in[:, :, 0:B], hpre[:], ACT.Gelu).then_inc(h_done, 1)
            copy_y(1, 2 * GROUPS, products((1, 7), GROUPS))
            copy_burst(LAST)
            copy_sums(2 * GROUPS, LAST + 2)
            round_y(1, 2 * GROUPS, GROUPS)
            for b in range(B):
                act.wait_ge(pick_done, b + 1)
                nc.scalar.activation(bcast[:, b, :], mxp[b % 2][:], ACT.Copy).then_inc(bcast_done, 1)

        @block.vector
        def _(dve):
            links = {"n": 0}

            def link(ins, base):
                links["n"] += 1
                ins.then_inc(link_s, 1)
                dve.wait_ge(link_s, base + links["n"])

            def bc(ap, n):
                return ap.unsqueeze(2).to_broadcast([ap.shape[0], ap.shape[1], n])

            def rows(ap):
                return ap.unsqueeze(1).to_broadcast([P, KT, B])

            def layernorm_sum():
                nc.vector.tensor_reduce(s1[:], th[:].rearrange("p k r -> p r k"), AX.X, ALU.add).then_inc(ln_sum, 1)

            def layernorm_centre(tu, base):
                dve.wait_ge(tr_full, tu + 1)
                nc.vector.tensor_tensor(cen[:], th[:], rows(trp[:, 0:B]), ALU.subtract).then_inc(tr_free, 1)
                dve.wait_ge(tr_free, tu + 2)
                link(nc.vector.tensor_tensor(sq[:], cen[:], cen[:], ALU.mult), base)
                nc.vector.tensor_reduce(s2[:], sq[:].rearrange("p k r -> p r k"), AX.X, ALU.add).then_inc(ln_sum, 1)

            def layernorm_scale(tu, k, base):
                dve.wait_ge(tr_full, tu + 2)
                nc.vector.tensor_scalar(ve[:], trp[:, 0:B], EPS_F, None, ALU.add).then_inc(ln_ve, 1)
                dve.wait_ge(ln_rs, k + 1)
                nc.vector.tensor_tensor(cen[:], cen[:], rows(rs[:]), ALU.mult).then_inc(tr_free, 1)
                dve.wait_ge(tr_free, tu + 3)
                link(nc.vector.tensor_tensor(cen[:], cen[:], bc(fvec[:, 1, :], B), ALU.mult), base)
                nc.vector.tensor_tensor(t_in[:, :, 0:B], cen[:], bc(fvec[:, 2, :], B), ALU.add).then_inc(t_done, 1)

            def row_max(k, count, par):
                i, h, per = MX[k]
                dve.wait_ge(mx_done, count + 1)
                bank, w = mxp[k % 2], (i + 1) * P
                src = bank[:].rearrange("p (h s) -> p h s", h=per)[:, :, 0:w]
                nc.vector.tensor_reduce(mx[par][:, i, h:h + per], src, AX.X, ALU.max, negate=True).then_inc(mx_free, 1)

            def add_burst(tu):
                dve.wait_ge(tr_full, tu + 1)
                nc.vector.tensor_tensor(fsb[:], trp[:], fsb[:], ALU.add).then_inc(tr_free, 1)

            def chunk_out(tu, base):
                dve.wait_ge(tr_full, tu + 1)
                v = trp[:].rearrange("p (c n k r) -> p n c r k", c=4, n=2, k=2)
                for nb in range(2):
                    last = nc.vector.tensor_reduce(fr[:, 4 * nb:4 * nb + 4, :], v[:, nb, :, 0:B, :], AX.X, ALU.add)
                last.then_inc(tr_free, 1)
                dve.wait_ge(tr_free, tu + 2)

            def reciprocals(quarter, k, tu):
                if quarter == 0:
                    dve.wait_ge(tr_free, tu + 2)
                    dve.wait_ge(yf_done, k + 1)
                cols = slice(quarter * P, (quarter + 1) * P)
                last = nc.vector.reciprocal(rinv[:, cols], sm[:, cols])
                if quarter == 3:
                    last.then_inc(rc_done, 1)

            def divide(half, k):
                dve.wait_ge(ys_done, k + 2)
                dve.wait_ge(y2_done, k + 1)
                dve.wait_ge(rc_done, k + 1)
                nc.vector.tensor_tensor(yf[:], ys[half][:], rinv[:], ALU.mult).then_inc(yf_done, 1)

            def rest_y(half, k):
                dve.wait_ge(y1_done, k + 1)
                nc.vector.tensor_tensor(y2[half][:], yf[:], f32(y1[half][:]), ALU.subtract).then_inc(y2_done, 1)

            for w, v in ((st_done, 1), (pv_done, 1), (add_done, 1), (ys_done, 1), (yf_done, 1), (y2_done, 1), (tr_free, 1), (act_done, 2),
                         (y_out[0], 1), (y_out[1], 1)):
                dve.sem_inc(w, v)

            dve.wait_ge(xl_in, 16)
            for k, eps in enumerate((EPS_X, EPS_F)):
                for cc in range(2):
                    last = nc.vector.bn_stats(lst[:, cc, :], xl[:, cc * 512:(cc + 1) * 512])
                link(last, 0)
                link(nc.vector.bn_aggr(lmv[:], lst[:].rearrange("p a b -> p (a b)")), 0)
                nc.vector.tensor_scalar(lve[:], lmv[:, 1:2], eps, None, ALU.add).then_inc(l_ve, 1)
                dve.wait_ge(l_rs, k + 1)
                link(nc.vector.tensor_scalar(xl, xl, lmv[:, 0:1], lrs[:], ALU.subtract, ALU.mult), 0)
            dve.wait_ge(gb_in, 128)
            link(nc.vector.tensor_tensor(xl, xl, gl, ALU.mult), 0)
            nc.vector.tensor_tensor(xl, xl, bl, ALU.add).then_inc(t_done, 1)
            nc.vector.memset(pr[1][:, :, PROB_W[1] - 768:], 1.0).then_inc(init_p, 1)

            steps = {MX_HALF: 0, 9: 1, 12: 2, 14: 3, 16: 4}
            for k in range(MX_LATE + 1):
                step = steps.get(k)
                if step == 0:
                    dve.wait_ge(tr_full, 1)
                    dve.wait_ge(init, 4)
                    nc.vector.tensor_copy(t_in[:, :, 0:B], trp[:, 0:KT * B].rearrange("p (k r) -> p k r", r=B)
                                          ).then_inc(tr_free, 1)
                elif step == 1:
                    add_burst(3)
                elif step == 2:
                    chunk_out(4, 0)
                    dve.wait_ge(c_in, 16 * 12)
                    link(nc.vector.tensor_tensor(th[:], fr[:], bc(fvec[:, 0, :], B), ALU.add), 0)
                    layernorm_sum()
                elif step == 3:
                    layernorm_centre(5, 0)
                elif step == 4:
                    layernorm_scale(5, 0, 0)
                if k < MX_LATE:
                    row_max(k, k, 0)
            BASE = links["n"]
            with dve.Fori(0, STEPS) as s:
                with dve.Fori(0, CH) as c:
                    links["n"] = 0
                    it = s * CH + c
                    base = it * LINKS_TURN + s * LINKS_STEP + BASE
                    for par in range(2):
                        n = it * 2 + par
                        tb = trb(s, c, par)
                        for slot in PLAN:
                            for e in slot:
                                k = 2 * n + 1 - e[1] if len(e) > 1 else None
                                if e[0] == "mx":
                                    ahead = e[1] < MX_LATE
                                    row_max(e[1], (n + ahead) * NMX + e[1], 1 - par if ahead else par)
                                elif e[0] == "rc":
                                    reciprocals(e[2], k, tb + use[("ss", e[1])])
                                elif e[0] == "ym":
                                    divide(e[1], k)
                                elif e[0] == "y2":
                                    rest_y(e[1], k)
                                elif e[0] == "fs":
                                    add_burst(tb + use["fb"])
                                elif e[0] == "ft":
                                    chunk_out(tb + use["ft"], base)
                                    if par == 0:
                                        dve.wait_ge(b1_in, (it + 1) * 16)
                                        nc.vector.tensor_tensor(hpre[:], fr[:], bc(b1c[:], B), ALU.add).then_inc(hp_done, 1)
                                    else:
                                        link(nc.vector.tensor_tensor(th[:], th[:], fr[:], ALU.add), base)
                    assert links["n"] == LINKS_TURN, links["n"]
                links["n"] = 0
                base = (s + 1) * (CH * LINKS_TURN) + s * LINKS_STEP + BASE
                link(nc.vector.tensor_tensor(th[:], th[:], bc(fvec[:, 3, :], B), ALU.add), base)
                tu = TR0 + s * TR_STEP + NT * TRN
                layernorm_sum()
                layernorm_centre(tu, base)
                layernorm_scale(tu, s + 1, base)
                assert links["n"] == LINKS_STEP, links["n"]
            nc.vector.tensor_copy(h_in[:, :, 0:B], th[:]).then_inc(t_done, 1)
            add_burst(LAST + 1)
            dve.wait_ge(tr_free, LAST + 3)
            nc.vector.tensor_tensor(fsb[:], fsb[:], fbias[:], ALU.add).then_inc(t_done, 1)
            for quarter in range(4):
                reciprocals(quarter, 2 * GROUPS, LAST + 2)
            divide(1, 2 * GROUPS)
            rest_y(1, 2 * GROUPS)

        @block.tensor
        def _(pe):
            def scores_max(k, count, par, first=False):
                i, h0, per = MX[k]
                if not first:
                    pe.wait_ge(mx_free, count - 1)
                bank, step = mxp[k % 2], 2 * HALF // per
                for hh in range(per):
                    lhs = qs[par][0:QR, h0 + hh, i * P:(i + 1) * P]
                    if per == 1:
                        nc.tensor.matmul(bank[:, 0:512], lhs, ks[par][0:QR, 0:512], start=True, stop=True)
                        w = [256, 256, 384, 512][i - 4]
                        nc.tensor.matmul(bank[:, 512:512 + w], lhs, ks[par][0:QR, 512:512 + w], start=True, stop=False)
                    else:
                        w = [256, 256, 384, 512][i]
                        nc.tensor.matmul(bank[:, hh * step:hh * step + w], lhs, ks[par][0:QR, 0:w], start=True, stop=False)
                    at = hh * step + i * P
                    last = nc.tensor.matmul(bank[:, at:at + P], ident16[:], mask_q[:], start=False, stop=True)
                last.then_inc(mx_done, 1)

            def scores(u, count, par):
                half, h, (segs, masks, _, _) = ST[u]
                pe.wait_ge(act_done, count + 1)
                for k, (j, q0, w, at) in enumerate(segs):
                    last = nc.tensor.matmul(stp[u % 2][:, at:at + w], ks[par][:, j * P:(j + 1) * P],
                                            qs[par][:, h, q0:q0 + w], start=True, stop=not masks)
                    if masks:
                        last = nc.tensor.matmul(stp[u % 2][:, masks[k]:masks[k] + P], ident16[:], mask_k[:],
                                                start=False, stop=True)
                last.then_inc(st_done, 1)

            def values(half, j, par):
                at, c0 = prob_piece(half, j)
                for h in range(REP):
                    last = nc.tensor.matmul(yp[h * HD:(h + 1) * HD, c0:HALF], vs[par][:, j, :],
                                            pr[half][:, h, at:at + HALF - c0], start=(j == 0), stop=(j == 4 * half + 3))
                last.then_inc(pv_done, 1)

            def prob_sums(half, j, tu):
                if j == SUMS[half][0]:
                    fill(tu)
                src, c0, c1 = (pr[0], 0, P) if j == 0 else (acc, 0, HALF) if half == 1 else (acc0, P, HALF)
                for h in range(REP):
                    last = nc.tensor.matmul(trp[h * HD:(h + 1) * HD, c0:c1], ones[:], src[:, h, 0:c1 - c0],
                                            start=True, stop=True)
                if j == SUMS[half][-1]:
                    last.then_inc(tr_full, 1)

            def fill(tu):
                pe.wait_ge(tr_free, tu + 1)

            def max_transpose(half, tu, par):
                fill(tu)
                for i in range(4):
                    last = nc.tensor.transpose(trp[0:REP, i * P:(i + 1) * P], mx[par][:, half * 4 + i, :], ident[:])
                last.then_inc(tr_full, 1)

            def burst(which, tu, src, calls, parts=(0, 1)):
                if parts[0] == 0:
                    fill(tu)
                    pe.wait_ge(w_in[which], calls)
                for kk in parts:
                    for nb in range(2):
                        for kh in range(2):
                            r = 32 * (2 * nb + kh)
                            last = nc.tensor.matmul(trp[r:r + 32, :], src[:, kh * 4 + which * 2 + kk, :],
                                                    wch[which][:, 2 * kh + kk, nb * HALF:(nb + 1) * HALF],
                                                    start=(kk == 0), stop=(kk == 1))
                if parts[-1] == 1:
                    last.then_inc(tr_full, 1)

            def burst_transpose(tu):
                fill(tu)
                for cc in range(4):
                    last = nc.tensor.transpose(trp[:, cc * P:(cc + 1) * P], fsb[:, cc * P:(cc + 1) * P], ident[:])
                last.then_inc(tr_full, 1)

            def mean(tu, v, count):
                fill(tu)
                pe.wait_ge(ln_sum, count)
                nc.tensor.matmul(trp[:, 0:B], onesd[:], v[:], start=True, stop=True).then_inc(tr_full, 1)

            def x_last():
                pe.wait_ge(t_done, 1)
                fill(0)
                for k in range(KT):
                    last = nc.tensor.transpose(trp[:, k * B:(k + 1) * B], xl[:, k * P:(k + 1) * P], ident[0:B, 0:B])
                last.then_inc(tr_full, 1)

            pe.wait_ge(qk_in[0], 80)
            for k in range(MX_LATE):
                if k == MX_HALF:
                    x_last()
                    pe.wait_ge(mx_free, MX_HALF)
                    max_transpose(0, 1, 0)
                elif k == 8:
                    burst(0, 2, t_in, 32)
                elif k == 9:
                    burst(1, 3, t_in, 32)
                elif k == 11:
                    burst_transpose(4)
                elif k == 13:
                    mean(5, s1, 1)
                elif k == 15:
                    mean(6, s2, 2)
                scores_max(k, k, 0, first=k < 2)
            pe.wait_ge(init, 8)
            pe.wait_ge(init_p, 2)
            for h in range(REP):
                nc.tensor.matmul(yp[h * HD:(h + 1) * HD, :], ones[:], acc[:, h, :], start=True, stop=False)
            with pe.Fori(0, STEPS) as s:
                with pe.Fori(0, CH) as c:
                    for par in range(2):
                        it = s * CH + c
                        n = it * 2 + par
                        tb = trb(s, c, par)
                        for u in range(NST):
                            if u == 0:
                                pe.wait_ge(m_in[par], (it + 1) * 16)
                            if u == HALF_ST:
                                pe.wait_ge(m_in[2 + par], (it + 1) * 16)
                            scores(u, n * NST + u, par)
                            for e in PLAN[u]:
                                if e[0] == "pv":
                                    _, half, j = e
                                    if e[1:] in CARRIED:
                                        pe.wait_ge(act_done, n * NST + 2)
                                        values(half, j, 1 - par)
                                        continue
                                    pe.wait_ge(act_done, n * NST + LAST_UNIT[(half, j)] + 3)
                                    if j == 0:
                                        pe.wait_ge(ys_done, 2 * n + half + 2)
                                    if (half, j) == (0, 0):
                                        pe.wait_ge(v_in[par], (it + 1) * 16)
                                    values(half, j, par)
                                elif e[0] == "ss":
                                    if e[1:] == (1, -1):
                                        pe.wait_ge(add_done, NADD * n + 4)
                                    if e[1:] == (0, -1):
                                        pe.wait_ge(add0_done, 3 * n + 3)
                                    prob_sums(e[1], e[2], tb + use[("ss", e[1])])
                                elif e[0] == "mx":
                                    ahead = e[1] < MX_LATE
                                    if e[1] == 0:
                                        pe.wait_ge(qk_in[1 - par], (it + 1 + par) * 80)
                                    scores_max(e[1], (n + ahead) * NMX + e[1], 1 - par if ahead else par)
                                elif e[0] == "mt":
                                    if e[1] == 1:
                                        pe.wait_ge(mx_free, (n + 1) * NMX)
                                        max_transpose(1, tb + use[e], par)
                                    else:
                                        pe.wait_ge(mx_free, (n + 1) * NMX + MX_HALF)
                                        max_transpose(0, tb + use[e], 1 - par)
                                elif e[0] in ("fa", "fb"):
                                    if e == ("fa", 0) and par == 0:
                                        pe.wait_ge(t_done, s + 2)
                                    elif e == ("fa", 0):
                                        pe.wait_ge(h_done, it + 1)
                                    burst(0 if e[0] == "fa" else 1, tb + use[e[0]], h_in if par else t_in,
                                          (n + 2) * 32, parts=e[1:])
                                elif e[0] == "ft":
                                    burst_transpose(tb + use["ft"])
                for k, v in enumerate((s1, s2)):
                    mean(TR0 + s * TR_STEP + NT * TRN + k, v, (s + 1) * 2 + k + 1)
            pe.wait_ge(act_done, GROUPS * NST + 2)
            values(1, 6, 1)
            values(1, 7, 1)
            pe.wait_ge(t_done, STEPS + 3)
            burst(0, LAST, h_in, (GROUPS + 2) * 32)
            burst(1, LAST + 1, h_in, (GROUPS + 2) * 32)
            pe.wait_ge(add_done, NADD * GROUPS + 4)
            prob_sums(1, -1, LAST + 2)
            pe.wait_ge(mx_free, GROUPS * NMX + MX_LATE)
            pe.wait_ge(c_in, 16 * 13)
            pe.wait_ge(t_done, STEPS + 4)
            for b in range(B):
                if b >= 2:
                    pe.wait_ge(bcast_done, b - 1)
                for nb in range(2):
                    last = nc.tensor.matmul(mxp[b % 2][:, nb * HALF:(nb + 1) * HALF], picks[:, (2 * b + nb) * P:(2 * b + nb + 1) * P],
                                            fsb[:], start=True, stop=True)
                last.then_inc(pick_done, 1)


MT1_OUT, MT0_OUT = 7, 28
ADD_AT = {19: 1, 23: 2, 27: 3, 31: 4}
ADD_LATE = 8
ADD_FIRST = 12
LINKS_TURN = 1
LINKS_STEP = 3


def output_phase(nc, x, woT, gate_w, gate_b, out_g, out_b, xt_d, y_d, mhalf, bcast, out):
    TILES = B * NT
    with ExitStack() as ctx:
        def sb(name, shape, dt):
            return ctx.enter_context(nc.sbuf_tensor(name, shape, dt))

        def ps(name, shape, dt):
            return ctx.enter_context(nc.psum_tensor(name, shape, dt))

        def sem(name):
            return ctx.enter_context(nc.semaphore(name))

        g1, g2 = (sb(f"g{i}", [P, KT, D], F32R) for i in (1, 2))
        o1, o2 = (sb(f"o{i}", [P, KT, D], F32R) for i in (1, 2))
        xa = [sb(f"xa{i}", [P, KT, P], F32R) for i in range(2)]
        ya = [sb(f"ya{i}", [P, KT, P], F32R) for i in range(2)]
        xs = [sb(f"xs{i}", [P, D], F32) for i in range(2)]
        a = [sb(f"a{i}", [P, D], F32) for i in range(2)]
        c = [sb(f"c{i}", [P, D], F32) for i in range(2)]
        wst = a + c
        NW = len(wst)
        vecs = sb("vecs", [P, 3, D], F32)
        bst = sb("o_bst", [P, 2, 6], F32)
        mv = sb("o_mv", [P, 2], F32)
        ve = sb("o_ve", [P, 1], F32)
        rstd = sb("o_rstd", [P, 2], F32)
        gp = [ps(f"gp{i}", [P, D], F32) for i in range(2)]
        op = [ps(f"op{i}", [P, D], F32) for i in range(2)]

        w_in = [sem(f"o_w_in{i}") for i in range(NW)]
        w1_done, w2_done, vec_in = sem("o_w1"), sem("o_w2"), sem("o_vec_in")
        xa_in, ya_in, xs_in, out_done = sem("o_xa_in"), sem("o_ya_in"), sem("o_xs_in"), [sem(f"o_out{i}") for i in range(2)]
        g_done, o_done, issue, issue_v = sem("o_g"), sem("o_o"), sem("o_issue"), sem("o_issue_v")
        link_s, ve_done, rstd_done = sem("o_link"), sem("o_ve_done"), sem("o_rstd_done")
        gb_done, gate_done, z_done, sig_done, a_done, o_free = (
            sem(f"o_{i}") for i in ("gb", "gate", "z", "sig", "a", "o_free"))
        block = ctx.enter_context(nc.Block())
        pieces = [(gate_w, g1, g2, k) for k in range(KT)] + [(woT, o1, o2, k) for k in range(KT)]

        @block.sync
        def _(sp):
            def load_x(n):
                return x[bass.ds(n * P, P), :]

            for n, (src, _, w2, k) in enumerate(pieces):
                sp.dma_start(wst[n % NW][:], src[k * P:(k + 1) * P, :]).then_inc(w_in[n % NW], 16)
                if n == KT + 1:
                    for r, v in enumerate((gate_b, out_g, out_b)):
                        sp.dma_start(vecs[:, r, :], v.partition_broadcast(P)).then_inc(vec_in, 16)
                    sp.dma_start(xs[0][:], x[0:P, :]).then_inc(xs_in, 16)
                if n >= NW - 1:
                    sp.wait_ge(w2_done, n - NW + 2)
            with sp.Fori(0, TILES // 2) as m:
                for par in range(2):
                    n = m * 2 + par
                    nn = (n + 1) % TILES
                    sp.wait_ge(out_done[1 - par], m * 16 + 1 if par == 0 else m * 16 + 17)
                    sp.dma_start(xs[1 - par][:], load_x(nn)).then_inc(xs_in, 16)
                    sp.wait_ge(a_done, n + 1)
                    sp.dma_start(out[bass.ds(n * P, P), :], a[par][:]).then_inc(out_done[par], 16)
            for par in range(2):
                sp.wait_ge(out_done[par], 16 * (TILES // 2) + 1)
            sp.wait_ge(xs_in, 16 * (TILES + 1))

        @block.gpsimd
        def _(pool):
            def load_xa(nn):
                pool.sem_inc(issue, 1)
                for part in range(2):
                    nc.gpsimd.dma_start(xa[part][:], xt_d[bass.ds(nn // NT, 1), part, :, :, bass.ds((nn % NT) * P, P)]
                                        .rearrange("a p k t -> (a p) k t")).then_inc(xa_in, 16)

            def load_ya(nn):
                pool.sem_inc(issue, 1)
                for part in range(2):
                    nc.gpsimd.dma_start(ya[part][:], y_d[part, bass.ds(1 + (nn // NT) * KV, KV), :, bass.ds((nn % NT) * P, P)]
                                        .rearrange("g p t -> p g t")).then_inc(ya_in, 16)

            def power(n, k):
                pool.wait_ge(ve_done, n * 2 + k + 1)
                nc.gpsimd.tensor_tensor(rstd[:, k:k + 1], ve[:], mhalf[:, 0:1], ALU.pow).then_inc(rstd_done, 1)

            load_xa(0)
            pool.wait_ge(w1_done, KT // 2)
            load_ya(0)
            with pool.Fori(0, TILES) as n:
                pool.wait_ge(g_done, n + 1)
                load_xa((n + 1) % TILES)
                power(n, 0)
                power(n, 1)
                pool.wait_ge(o_done, n + 1)
                load_ya((n + 1) % TILES)
            pool.wait_ge(xa_in, 32 * (TILES + 1))
            pool.wait_ge(ya_in, 32 * (TILES + 1))

        @block.scalar
        def _(act):
            for n, (_, w1, w2, k) in enumerate(pieces):
                act.wait_ge(w_in[n % NW], 16 * (n // NW + 1))
                nc.scalar.activation(w1[:, k, :], wst[n % NW][:], ACT.Copy).then_inc(w1_done, 1)
            with act.Fori(0, TILES // 2) as m:
                for par in range(2):
                    n = m * 2 + par
                    act.wait_ge(gb_done, n + 1)
                    nc.scalar.activation(c[par][:], a[par][:], ACT.Sigmoid).then_inc(gate_done, 1)
                    act.wait_ge(z_done, n + 1)
                    nc.scalar.activation(c[par][:], a[par][:], ACT.Sigmoid).then_inc(sig_done, 1)

        @block.vector
        def _(dve):
            for w, v in ((out_done[0], 1), (out_done[1], 1), (o_free, 2)):
                dve.sem_inc(w, v)
            for n, (_, w1, w2, k) in enumerate(pieces):
                dve.wait_ge(w1_done, n + 1)
                nc.vector.tensor_tensor(w2[:, k, :], wst[n % NW][:], f32(w1[:, k, :]), ALU.subtract).then_inc(w2_done, 1)
            dve.wait_ge(w2_done, 2 * KT)
            dve.wait_ge(vec_in, 48)
            LINKS = 10
            with dve.Fori(0, TILES // 2) as m:
                for par in range(2):
                    n = m * 2 + par
                    A, C, X = a[par], c[par], xs[par]
                    count = {"n": 0}

                    def link(ins):
                        count["n"] += 1
                        ins.then_inc(link_s, 1)
                        dve.wait_ge(link_s, n * LINKS + count["n"])

                    def stats(src, eps, which):
                        for cc in range(2):
                            last = nc.vector.bn_stats(bst[:, cc, :], src[:, cc * 512:(cc + 1) * 512])
                        link(last)
                        dve.sem_inc(issue_v, 1)
                        link(nc.vector.bn_aggr(mv[:], bst[:].rearrange("p a b -> p (a b)")))
                        nc.vector.tensor_scalar(ve[:], mv[:, 1:2], eps, None, ALU.add).then_inc(ve_done, 1)
                        dve.wait_ge(rstd_done, 2 * n + which + 1)

                    dve.wait_ge(g_done, n + 1)
                    dve.wait_ge(out_done[par], m * 16 + 1)
                    nc.vector.tensor_tensor(A[:], gp[par][:], vecs[:, 0, :], ALU.add).then_inc(gb_done, 1)
                    dve.wait_ge(xs_in, 16 * (n + 1))
                    stats(X, EPS_X, 0)
                    dve.wait_ge(gate_done, n + 1)
                    link(nc.vector.tensor_scalar(A[:], X[:], mv[:, 0:1], rstd[:, 0:1], ALU.subtract, ALU.mult))
                    link(nc.vector.tensor_tensor(C[:], C[:], bcast[:, bass.ds(n // NT, 1), :]
                                                 .rearrange("p a d -> p (a d)"), ALU.mult))
                    link(nc.vector.tensor_tensor(A[:], A[:], C[:], ALU.add))
                    stats(A, EPS_F, 1)
                    link(nc.vector.tensor_scalar(A[:], A[:], mv[:, 0:1], rstd[:, 1:2], ALU.subtract, ALU.mult))
                    link(nc.vector.tensor_tensor(A[:], A[:], vecs[:, 1, :], ALU.mult))
                    nc.vector.tensor_tensor(A[:], A[:], vecs[:, 2, :], ALU.add).then_inc(z_done, 1)
                    dve.wait_ge(o_done, n + 1)
                    dve.wait_ge(z_done, n + 1)
                    dve.wait_ge(sig_done, n + 1)
                    link(nc.vector.tensor_tensor(A[:], A[:], C[:], ALU.mult))
                    nc.vector.tensor_tensor(A[:], op[par][:], A[:], ALU.mult).then_inc(o_free, 1)
                    dve.wait_ge(o_free, n + 3)
                    nc.vector.tensor_tensor(A[:], A[:], X[:], ALU.add).then_inc(a_done, 1)
                    assert count["n"] == LINKS, count

        @block.tensor
        def _(pe):
            def product(bank, lhs, ws, first):
                for k in range(KT):
                    for pa, pw in ((0, 0), (1, 0), (0, 1)):
                        if first is not None and pa == 0 and pw == 0:
                            pe.wait_ge(w2_done, first + k + 1)
                        for half in range(2):
                            cols = slice(half * HALF, (half + 1) * HALF)
                            last = nc.tensor.matmul(bank[:, cols], lhs[pa][:, k, :], ws[pw][:, k, cols],
                                                    start=(k == 0 and (pa, pw) == (0, 0)),
                                                    stop=(k == KT - 1 and (pa, pw) == (0, 1)))
                return last

            def tile(n, par, first):
                pe.wait_ge(xa_in, 32 * (n + 1))
                if not first:
                    pe.wait_ge(gb_done, n - 1)
                product(gp[par], xa, (g1, g2), 0 if first else None).then_inc(g_done, 1)
                pe.wait_ge(ya_in, 32 * (n + 1))
                pe.wait_ge(o_free, n + 1)
                product(op[par], ya, (o1, o2), KT if first else None).then_inc(o_done, 1)

            tile(0, 0, True)
            tile(1, 1, True)
            with pe.Fori(1, TILES // 2) as m:
                for par in range(2):
                    tile(m * 2 + par, par, False)


def pair_rows(w, heads):
    w = np.asarray(w).reshape(heads // 8, 8, EO, 2, D)
    return np.ascontiguousarray(w.transpose(4, 0, 3, 2, 1).reshape(D, heads * HD))


def columns(v):
    return np.ascontiguousarray(np.asarray(v).reshape(-1, P).T)


def rope_tables():
    theta = np.float32(1.0) / np.power(np.float32(10000.0), np.arange(0, HD, 2, dtype=np.float32) / np.float32(HD))
    freqs = np.arange(T, dtype=np.float32)[None, :] * theta.astype(np.float32)[:, None]
    return [np.ascontiguousarray(np.repeat(f(freqs).astype(np.float32), 8, axis=0)) for f in (np.cos, np.sin)]


def row_picks():
    pick = np.zeros((P, 2 * B, P), np.float32)
    for b in range(B):
        for nb in range(2):
            for kh in range(2):
                pick[32 * (2 * nb + kh) + b, 2 * b + nb] = 1.0
    return pick


def kernel(**inputs):
    import concourse.bacc as _bacc
    from concourse.bass_utils import run_bass_kernel_spmd as _run

    a = {k: np.asarray(v) for k, v in inputs.items()}
    f = {k.removeprefix("L0_ffn_").removeprefix("L0_attn_"): v for k, v in a.items()}
    rope_c, rope_s = rope_tables()
    row = lambda v: np.ascontiguousarray(v.reshape(1, -1))
    arrays = {
        "x": np.ascontiguousarray(f["x"].reshape(B * T, D)),
        "wqT": pair_rows(f["wq"], H), "wkT": pair_rows(f["wk"], KV),
        "wvT": np.ascontiguousarray(f["wv"].T), "woT": np.ascontiguousarray(f["wo"].T),
        "in_g": row(f["in_gamma"]), "in_b": row(f["in_beta"]),
        "agg_w": f["agg_w"], "agg_b": columns(f["agg_b"]),
        "pn_g": columns(f["pn_gamma"]), "pn_b": columns(f["pn_beta"]),
        "d1_w": np.concatenate([f["d1_w"], f["bc_w"]], axis=1),
        "d1_b": np.ascontiguousarray(f["d1_b"].reshape(CH, KT, P).transpose(0, 2, 1)),
        "d2_w": f["d2_w"], "d2_b": columns(f["d2_b"]), "bc_b": row(f["bc_b"]),
        "gate_w": f["gate_w"], "gate_b": row(f["gate_b"]), "out_g": row(f["out_gamma"]), "out_b": row(f["out_beta"]),
        "rope_c": rope_c, "rope_s": rope_s, "pick": row_picks().reshape(P, 2 * B * P),
    }
    nc = _bacc.Bacc("TRN2", target_bir_lowering=False, num_devices=1)
    named, aps = {}, {}
    for name, v in arrays.items():
        named[f"in_{name}"] = np.ascontiguousarray(v)
        aps[name] = nc.dram_tensor(f"in_{name}", v.shape, mybir.dt.from_np(v.dtype), kind="ExternalInput").ap()
    aps["out"] = nc.dram_tensor("out", (B * T, D), F32, kind="ExternalOutput").ap()
    build_kernel(nc, **aps)
    r = _run(nc, [named], core_ids=[0])
    return r.results[0]["out"].reshape(B, T, D)
```
